# Optimizing a Trainium2 kernel written in Bass

```python
import numpy as np
import jax
import jax.numpy as jnp

def _softmax(x, axis=-1):
    return jax.nn.softmax(x, axis=axis)

def _gelu(x):
    return jax.nn.gelu(x, approximate=True)

def _silu(x):
    return jax.nn.silu(x)

def _sigmoid(x):
    return jax.nn.sigmoid(x)

def _layernorm(x, axis=-1, eps=1e-05):
    m = jnp.mean(x, axis=axis, keepdims=True)
    v = jnp.var(x, axis=axis, keepdims=True)
    return (x - m) / jnp.sqrt(v + eps)

def _scatter_add(tgt, idx, src, axis=0):
    return tgt.at[idx].add(src)

def _segment_sum(src, seg, n):
    return jax.ops.segment_sum(src, seg, n)
kernel_name = 'mk_gps_d2_gnn_r8_3ff223'

def setup_inputs(seed: int=0):
    np.random.seed(seed)
    _w = jnp.asarray

    def _rec_inputs():
        import jax
        import jax.numpy as jnp
        _gk = jax.random.key(seed)
        x = -0.0003713 + 1 * jax.random.normal(jax.random.fold_in(_gk, 1), (6250, 256), jnp.float32)
        src = jax.random.randint(jax.random.fold_in(_gk, 2), (100000,), 0, 6250, jnp.int32)
        dst = jax.random.randint(jax.random.fold_in(_gk, 3), (100000,), 0, 6250, jnp.int32)
        _o = jnp.argsort(dst, stable=True)
        src = src[_o]
        dst = dst[_o]
        return (x, src, dst)
    x, src, dst = _rec_inputs()

    def _L0_gnn_setup():
        import jax, jax.numpy as jnp
        import numpy as np
        N, D, H, C = (6250, 256, 4, 16)
        E = 200000
        NEG_SLOPE = 0.2

        def _gatv2_layer(x, src, dst, Wl, bl, Wr, br, att, bias, n_nodes):
            xl = (x @ Wl + bl).reshape(n_nodes, H, C)
            xr = (x @ Wr + br).reshape(n_nodes, H, C)
            e = jax.nn.leaky_relu(xl[src] + xr[dst], negative_slope=NEG_SLOPE)
            logits = jnp.einsum('ehc,hc->eh', e, att)
            m = jax.ops.segment_max(logits, dst, num_segments=n_nodes)
            ex = jnp.exp(logits - m[dst])
            denom = jax.ops.segment_sum(ex, dst, num_segments=n_nodes)
            alpha = ex / denom[dst]
            out = jax.ops.segment_sum(alpha[:, :, None] * xl[src], dst, num_segments=n_nodes)
            return out.reshape(n_nodes, H * C) + bias
        key = jax.random.key(seed)
        ks = jax.random.split(key, 16)
        g = lambda k, shp, fan: jax.random.normal(k, shp, jnp.float32) * (1.0 / np.sqrt(fan))
        inp = {'x': jax.random.normal(ks[0], (N, D), jnp.float32), 'edge_index': jax.random.randint(ks[1], (2, E), 0, N, dtype=jnp.int64), 'Wl1': g(ks[2], (D, H * C), D), 'bl1': jnp.zeros((H * C,), jnp.float32), 'Wr1': g(ks[3], (D, H * C), D), 'br1': jnp.zeros((H * C,), jnp.float32), 'att1': g(ks[4], (H, C), C), 'bias1': jnp.zeros((H * C,), jnp.float32), 'Wl2': g(ks[5], (H * C, H * C), H * C), 'bl2': jnp.zeros((H * C,), jnp.float32), 'Wr2': g(ks[6], (H * C, H * C), H * C), 'br2': jnp.zeros((H * C,), jnp.float32), 'att2': g(ks[7], (H, C), C), 'bias2': jnp.zeros((H * C,), jnp.float32), 'Wo': g(ks[8], (H * C, D), H * C), 'bo': jnp.zeros((D,), jnp.float32)}
        return inp
    _L0_gnn_all = _L0_gnn_setup()
    _L0_gnn_in = {k: v for k, v in _L0_gnn_all.items() if k in ('Wl1', 'bl1', 'Wr1', 'br1', 'att1', 'bias1', 'Wl2', 'bl2', 'Wr2', 'br2', 'att2', 'bias2', 'Wo', 'bo')}
    del _L0_gnn_all

    def _L0_mix_setup():
        import jax, jax.numpy as jnp
        import numpy as np
        C_CURV = 1.0
        MIN_NORM = 1e-15
        BALL_EPS = 1e-05
        ATT_EPS = 1e-15
        DIM = 32

        def _norm(x):
            return jnp.clip(jnp.linalg.norm(x, axis=-1, keepdims=True), MIN_NORM)

        def proj(x, c):
            maxnorm = (1.0 - BALL_EPS) / jnp.sqrt(c)
            n = _norm(x)
            return jnp.where(n > maxnorm, x / n * maxnorm, x)

        def expmap0(u, c):
            sc = jnp.sqrt(c)
            n = _norm(u)
            return jnp.tanh(sc * n) * u / (sc * n)

        def logmap0(p, c):
            sc = jnp.sqrt(c)
            n = _norm(p)
            return jnp.arctanh(jnp.clip(sc * n, -1.0 + 1e-07, 1.0 - 1e-07)) * p / (sc * n)

        def mobius_add(x, y, c):
            x2 = jnp.sum(x * x, -1, keepdims=True)
            y2 = jnp.sum(y * y, -1, keepdims=True)
            xy = jnp.sum(x * y, -1, keepdims=True)
            num = (1 + 2 * c * xy + c * y2) * x + (1 - c * x2) * y
            den = 1 + 2 * c * xy + c * c * x2 * y2
            return num / jnp.clip(den, MIN_NORM)

        def conv1d(x, w, pad, groups=1):
            return jax.lax.conv_general_dilated(x, w, (1,), [(pad, pad)], dimension_numbers=('NCH', 'OIH', 'NCH'), feature_group_count=groups)

        def batchnorm(x, gamma, beta):
            mean = jnp.mean(x, axis=(0, 2), keepdims=True)
            var = jnp.var(x, axis=(0, 2), keepdims=True)
            xn = (x - mean) * jax.lax.rsqrt(var + 1e-05)
            return gamma[None, :, None] * xn + beta[None, :, None]

        def _reference_tuple_inner(x, w_qkv, bn_gamma, bn_beta, w_dw, w_pw, w_res, b_res):
            c = C_CURV
            h = logmap0(proj(x, c), c)
            h = jnp.transpose(h, (1, 2, 0))
            h = conv1d(h, w_qkv, pad=2)
            h = batchnorm(h, bn_gamma, bn_beta)
            h = jax.nn.relu(jnp.transpose(h, (2, 0, 1)))
            qkv = proj(expmap0(h, c), c)
            t = jnp.transpose(logmap0(proj(qkv, c), c), (1, 2, 0))
            s = conv1d(t, w_dw, pad=2, groups=t.shape[1])
            s = conv1d(s, w_pw, pad=0, groups=t.shape[1] // DIM)
            cat = jnp.concatenate([t, s], axis=1)
            ai = proj(expmap0(jnp.transpose(cat, (2, 0, 1)), c), c)
            t2 = logmap0(proj(ai, c), c)
            L, N, C2 = t2.shape
            g = C2 // (3 * DIM)
            qkv3 = jnp.transpose(t2, (1, 2, 0)).reshape(N, g, 3 * DIM, L)
            q, k, v = jnp.split(qkv3, 3, axis=2)
            q = jax.nn.relu(q)
            k = jax.nn.relu(k)
            vk = jnp.einsum('ngdl,ngel->ngde', v, k)
            out = jnp.einsum('ngde,ngdl->ngdl', vk, q)
            out = out / (jnp.sum(v, -1, keepdims=True) + ATT_EPS)
            out = jnp.transpose(out.reshape(N, g * DIM, L), (2, 0, 1))
            fx_h = proj(expmap0(out, c), c)
            ft = jnp.transpose(logmap0(proj(fx_h, c), c), (1, 2, 0))
            ft = conv1d(ft, w_res, pad=0) + b_res[None, :, None]
            fx = proj(expmap0(jnp.transpose(ft, (2, 0, 1)), c), c)
            residual = mobius_add(fx, x, c)
            return (fx, residual)
        key = jax.random.key(seed)
        ks = jax.random.split(key, 6)
        L, N, C, TD = (256, 16, 256, 256)
        x = jax.random.normal(ks[0], (L, N, C), jnp.float32) * 0.05
        w_qkv = jax.random.normal(ks[1], (3 * TD, C, 5), jnp.float32) / np.sqrt(C * 5)
        bn_gamma = jnp.ones((3 * TD,), jnp.float32)
        bn_beta = jnp.zeros((3 * TD,), jnp.float32)
        w_dw = jax.random.normal(ks[2], (3 * TD, 1, 5), jnp.float32) / np.sqrt(5.0)
        w_pw = jax.random.normal(ks[3], (3 * TD, DIM, 1), jnp.float32) / np.sqrt(DIM)
        w_res = jax.random.normal(ks[4], (C, 2 * TD, 1), jnp.float32) / np.sqrt(2 * TD)
        b_res = jnp.zeros((C,), jnp.float32)
        return {'x': x, 'w_qkv': w_qkv, 'bn_gamma': bn_gamma, 'bn_beta': bn_beta, 'w_dw': w_dw, 'w_pw': w_pw, 'w_res': w_res, 'b_res': b_res}
    _L0_mix_all = _L0_mix_setup()
    _L0_mix_in = {k: v for k, v in _L0_mix_all.items() if k in ('w_qkv', 'bn_gamma', 'bn_beta', 'w_dw', 'w_pw', 'w_res', 'b_res')}
    del _L0_mix_all

    def _L0_ffn_setup():
        import jax, jax.numpy as jnp
        import numpy as np
        B, S, D = (8, 512, 256)
        H = 4 * D
        CAPACITY = 0.5
        key = jax.random.key(seed)
        ks = jax.random.split(key, 6)
        x = jax.random.normal(ks[0], (B, S, D), dtype=jnp.float32)
        attention_mask = jnp.zeros((B, 1, 1, S), dtype=jnp.float32)
        wr = jax.random.normal(ks[1], (D, 1), dtype=jnp.float32) * 0.02
        br = jnp.zeros((1,), dtype=jnp.float32)
        w1 = jax.random.normal(ks[2], (D, H), dtype=jnp.float32) * 0.02
        b1 = jnp.zeros((H,), dtype=jnp.float32)
        w2 = jax.random.normal(ks[3], (H, D), dtype=jnp.float32) * 0.02
        b2 = jnp.zeros((D,), dtype=jnp.float32)
        return {'x': x, 'attention_mask': attention_mask, 'wr': wr, 'br': br, 'w1': w1, 'b1': b1, 'w2': w2, 'b2': b2}
    _L0_ffn_all = _L0_ffn_setup()
    _L0_ffn_in = {k: v for k, v in _L0_ffn_all.items() if k in ('attention_mask', 'wr', 'br', 'w1', 'b1', 'w2', 'b2')}
    del _L0_ffn_all

    def _L1_gnn_setup():
        import jax, jax.numpy as jnp
        import numpy as np
        N = 6250
        E = 100000
        D_IN = 256
        HID = 32
        HEADS = 8
        D_OUT = 64
        NEG_SLOPE = 0.2

        def _gat_conv(x, src, dst, W, att_src, att_dst, bias, heads, out_dim, concat):
            n = x.shape[0]
            h = (x @ W.T).reshape(n, heads, out_dim)
            a_s = jnp.sum(h * att_src, axis=-1)
            a_d = jnp.sum(h * att_dst, axis=-1)
            logits = jax.nn.leaky_relu(a_s[src] + a_d[dst], NEG_SLOPE)
            m = jax.ops.segment_max(logits, dst, num_segments=n)
            e = jnp.exp(logits - m[dst])
            den = jax.ops.segment_sum(e, dst, num_segments=n)
            alpha = e / (den[dst] + 1e-16)
            out = jax.ops.segment_sum(alpha[:, :, None] * h[src], dst, num_segments=n)
            out = out.reshape(n, heads * out_dim) if concat else out.mean(axis=1)
            return out + bias
        key = jax.random.key(seed)
        ks = jax.random.split(key, 12)
        x = jax.random.normal(ks[0], (N, D_IN), jnp.float32)
        edge_index = jax.random.randint(ks[1], (2, E), 0, N, dtype=jnp.int32)
        g = lambda k, shape, fan_in: jax.random.normal(k, shape, jnp.float32) / np.sqrt(fan_in)
        W0 = g(ks[2], (HEADS * HID, D_IN), D_IN)
        att_src0 = g(ks[3], (1, HEADS, HID), HID)
        att_dst0 = g(ks[4], (1, HEADS, HID), HID)
        b0 = jnp.zeros((HEADS * HID,), jnp.float32)
        W1 = g(ks[5], (1 * D_OUT, HEADS * HID), HEADS * HID)
        att_src1 = g(ks[6], (1, 1, D_OUT), D_OUT)
        att_dst1 = g(ks[7], (1, 1, D_OUT), D_OUT)
        b1 = jnp.zeros((D_OUT,), jnp.float32)
        return {'x': x, 'edge_index': edge_index, 'W0': W0, 'att_src0': att_src0, 'att_dst0': att_dst0, 'b0': b0, 'W1': W1, 'att_src1': att_src1, 'att_dst1': att_dst1, 'b1': b1}
    _L1_gnn_all = _L1_gnn_setup()
    _L1_gnn_in = {k: v for k, v in _L1_gnn_all.items() if k in ('W0', 'att_src0', 'att_dst0', 'b0', 'W1', 'att_src1', 'att_dst1', 'b1')}
    del _L1_gnn_all

    def _L1_mix_setup():
        import jax, jax.numpy as jnp
        import numpy as np
        A, Bc, Cc = (0.5, 1.0, 1.0)
        H = 8
        EPS = 1e-12

        def _normalize(t):
            n = jnp.linalg.norm(t, axis=-1, keepdims=True)
            return t / jnp.maximum(n, EPS)
        key = jax.random.key(seed)
        ks = jax.random.split(key, 5)
        B, N, C = (8, 256, 256)
        D = C // H
        x = jax.random.normal(ks[0], (B, N, C), dtype=jnp.float32)
        Wqkv = jax.random.normal(ks[1], (3 * H * D, C), dtype=jnp.float32) * 0.02
        bqkv = jnp.zeros((3 * H * D,), dtype=jnp.float32)
        Wproj = jax.random.normal(ks[2], (C, H * D), dtype=jnp.float32) * 0.02
        bproj = jnp.zeros((C,), dtype=jnp.float32)
        temperature = jnp.ones((1, H, 1, 1), dtype=jnp.float32)
        return {'x': x, 'Wqkv': Wqkv, 'bqkv': bqkv, 'Wproj': Wproj, 'bproj': bproj, 'temperature': temperature}
    _L1_mix_all = _L1_mix_setup()
    _L1_mix_in = {k: v for k, v in _L1_mix_all.items() if k in ('Wqkv', 'bqkv', 'Wproj', 'bproj', 'temperature')}
    del _L1_mix_all

    def _L1_ffn_setup():
        import jax, jax.numpy as jnp
        import numpy as np
        DIM = 256
        H = 8
        D = 64
        G = 64
        INNER = H * D
        SCALE = D ** (-0.5)
        key = jax.random.key(seed)
        ks = jax.random.split(key, 12)
        B, N = (4, 2048)
        x = jax.random.normal(ks[0], (B, N, DIM), dtype=jnp.float32)
        s = lambda fan_in: 1.0 / np.sqrt(fan_in)
        W_fx = jax.random.normal(ks[1], (DIM, INNER), dtype=jnp.float32) * s(DIM)
        b_fx = jnp.zeros((INNER,), dtype=jnp.float32)
        W_x = jax.random.normal(ks[2], (DIM, INNER), dtype=jnp.float32) * s(DIM)
        b_x = jnp.zeros((INNER,), dtype=jnp.float32)
        A = jax.random.normal(ks[3], (G, D), dtype=jnp.float32)
        Q, _ = jnp.linalg.qr(A.T)
        W_slice = Q[:, :G].astype(jnp.float32)
        b_slice = jnp.zeros((G,), dtype=jnp.float32)
        W_q = jax.random.normal(ks[4], (D, D), dtype=jnp.float32) * s(D)
        W_k = jax.random.normal(ks[5], (D, D), dtype=jnp.float32) * s(D)
        W_v = jax.random.normal(ks[6], (D, D), dtype=jnp.float32) * s(D)
        W_out = jax.random.normal(ks[7], (INNER, DIM), dtype=jnp.float32) * s(INNER)
        b_out = jnp.zeros((DIM,), dtype=jnp.float32)
        temperature = jnp.ones((1, H, 1, 1), dtype=jnp.float32) * 0.5
        return {'x': x, 'W_fx': W_fx, 'b_fx': b_fx, 'W_x': W_x, 'b_x': b_x, 'W_slice': W_slice, 'b_slice': b_slice, 'W_q': W_q, 'W_k': W_k, 'W_v': W_v, 'W_out': W_out, 'b_out': b_out, 'temperature': temperature}
    _L1_ffn_all = _L1_ffn_setup()
    _L1_ffn_in = {k: v for k, v in _L1_ffn_all.items() if k in ('W_fx', 'b_fx', 'W_x', 'b_x', 'W_slice', 'b_slice', 'W_q', 'W_k', 'W_v', 'W_out', 'b_out', 'temperature')}
    del _L1_ffn_all
    return {'x': x, 'src': src, 'dst': dst, 'L0_gnn_Wl1': _L0_gnn_in['Wl1'], 'L0_gnn_bl1': _L0_gnn_in['bl1'], 'L0_gnn_Wr1': _L0_gnn_in['Wr1'], 'L0_gnn_br1': _L0_gnn_in['br1'], 'L0_gnn_att1': _L0_gnn_in['att1'], 'L0_gnn_bias1': _L0_gnn_in['bias1'], 'L0_gnn_Wl2': _L0_gnn_in['Wl2'], 'L0_gnn_bl2': _L0_gnn_in['bl2'], 'L0_gnn_Wr2': _L0_gnn_in['Wr2'], 'L0_gnn_br2': _L0_gnn_in['br2'], 'L0_gnn_att2': _L0_gnn_in['att2'], 'L0_gnn_bias2': _L0_gnn_in['bias2'], 'L0_gnn_Wo': _L0_gnn_in['Wo'], 'L0_gnn_bo': _L0_gnn_in['bo'], 'L0_mix_w_qkv': _L0_mix_in['w_qkv'], 'L0_mix_bn_gamma': _L0_mix_in['bn_gamma'], 'L0_mix_bn_beta': _L0_mix_in['bn_beta'], 'L0_mix_w_dw': _L0_mix_in['w_dw'], 'L0_mix_w_pw': _L0_mix_in['w_pw'], 'L0_mix_w_res': _L0_mix_in['w_res'], 'L0_mix_b_res': _L0_mix_in['b_res'], 'L0_ffn_attention_mask': _L0_ffn_in['attention_mask'], 'L0_ffn_wr': _L0_ffn_in['wr'], 'L0_ffn_br': _L0_ffn_in['br'], 'L0_ffn_w1': _L0_ffn_in['w1'], 'L0_ffn_b1': _L0_ffn_in['b1'], 'L0_ffn_w2': _L0_ffn_in['w2'], 'L0_ffn_b2': _L0_ffn_in['b2'], 'L1_gnn_W0': _L1_gnn_in['W0'], 'L1_gnn_att_src0': _L1_gnn_in['att_src0'], 'L1_gnn_att_dst0': _L1_gnn_in['att_dst0'], 'L1_gnn_b0': _L1_gnn_in['b0'], 'L1_gnn_W1': _L1_gnn_in['W1'], 'L1_gnn_att_src1': _L1_gnn_in['att_src1'], 'L1_gnn_att_dst1': _L1_gnn_in['att_dst1'], 'L1_gnn_b1': _L1_gnn_in['b1'], 'L1_mix_Wqkv': _L1_mix_in['Wqkv'], 'L1_mix_bqkv': _L1_mix_in['bqkv'], 'L1_mix_Wproj': _L1_mix_in['Wproj'], 'L1_mix_bproj': _L1_mix_in['bproj'], 'L1_mix_temperature': _L1_mix_in['temperature'], 'L1_ffn_W_fx': _L1_ffn_in['W_fx'], 'L1_ffn_b_fx': _L1_ffn_in['b_fx'], 'L1_ffn_W_x': _L1_ffn_in['W_x'], 'L1_ffn_b_x': _L1_ffn_in['b_x'], 'L1_ffn_W_slice': _L1_ffn_in['W_slice'], 'L1_ffn_b_slice': _L1_ffn_in['b_slice'], 'L1_ffn_W_q': _L1_ffn_in['W_q'], 'L1_ffn_W_k': _L1_ffn_in['W_k'], 'L1_ffn_W_v': _L1_ffn_in['W_v'], 'L1_ffn_W_out': _L1_ffn_in['W_out'], 'L1_ffn_b_out': _L1_ffn_in['b_out'], 'L1_ffn_temperature': _L1_ffn_in['temperature']}

def reference(x, src, dst, L0_gnn_Wl1, L0_gnn_bl1, L0_gnn_Wr1, L0_gnn_br1, L0_gnn_att1, L0_gnn_bias1, L0_gnn_Wl2, L0_gnn_bl2, L0_gnn_Wr2, L0_gnn_br2, L0_gnn_att2, L0_gnn_bias2, L0_gnn_Wo, L0_gnn_bo, L0_mix_w_qkv, L0_mix_bn_gamma, L0_mix_bn_beta, L0_mix_w_dw, L0_mix_w_pw, L0_mix_w_res, L0_mix_b_res, L0_ffn_attention_mask, L0_ffn_wr, L0_ffn_br, L0_ffn_w1, L0_ffn_b1, L0_ffn_w2, L0_ffn_b2, L1_gnn_W0, L1_gnn_att_src0, L1_gnn_att_dst0, L1_gnn_b0, L1_gnn_W1, L1_gnn_att_src1, L1_gnn_att_dst1, L1_gnn_b1, L1_mix_Wqkv, L1_mix_bqkv, L1_mix_Wproj, L1_mix_bproj, L1_mix_temperature, L1_ffn_W_fx, L1_ffn_b_fx, L1_ffn_W_x, L1_ffn_b_x, L1_ffn_W_slice, L1_ffn_b_slice, L1_ffn_W_q, L1_ffn_W_k, L1_ffn_W_v, L1_ffn_W_out, L1_ffn_b_out, L1_ffn_temperature):
    import jax
    import jax.numpy as jnp

    def _L0_gnn_ref(x, edge_index, Wl1, bl1, Wr1, br1, att1, bias1, Wl2, bl2, Wr2, br2, att2, bias2, Wo, bo):
        import jax, jax.numpy as jnp
        import numpy as np
        N, D, H, C = (6250, 256, 4, 16)
        E = 200000
        NEG_SLOPE = 0.2

        def _gatv2_layer(x, src, dst, Wl, bl, Wr, br, att, bias, n_nodes):
            xl = (x @ Wl + bl).reshape(n_nodes, H, C)
            xr = (x @ Wr + br).reshape(n_nodes, H, C)
            e = jax.nn.leaky_relu(xl[src] + xr[dst], negative_slope=NEG_SLOPE)
            logits = jnp.einsum('ehc,hc->eh', e, att)
            m = jax.ops.segment_max(logits, dst, num_segments=n_nodes)
            ex = jnp.exp(logits - m[dst])
            denom = jax.ops.segment_sum(ex, dst, num_segments=n_nodes)
            alpha = ex / denom[dst]
            out = jax.ops.segment_sum(alpha[:, :, None] * xl[src], dst, num_segments=n_nodes)
            return out.reshape(n_nodes, H * C) + bias
        src, dst = (edge_index[0], edge_index[1])
        h = jax.nn.relu(_gatv2_layer(x, src, dst, Wl1, bl1, Wr1, br1, att1, bias1, N))
        h = jax.nn.relu(_gatv2_layer(h, src, dst, Wl2, bl2, Wr2, br2, att2, bias2, N))
        return jax.nn.sigmoid(h @ Wo + bo)

    def _L0_mix_ref(x, w_qkv, bn_gamma, bn_beta, w_dw, w_pw, w_res, b_res):
        import jax, jax.numpy as jnp
        import numpy as np
        C_CURV = 1.0
        MIN_NORM = 1e-15
        BALL_EPS = 1e-05
        ATT_EPS = 1e-15
        DIM = 32

        def _norm(x):
            return jnp.clip(jnp.linalg.norm(x, axis=-1, keepdims=True), MIN_NORM)

        def proj(x, c):
            maxnorm = (1.0 - BALL_EPS) / jnp.sqrt(c)
            n = _norm(x)
            return jnp.where(n > maxnorm, x / n * maxnorm, x)

        def expmap0(u, c):
            sc = jnp.sqrt(c)
            n = _norm(u)
            return jnp.tanh(sc * n) * u / (sc * n)

        def logmap0(p, c):
            sc = jnp.sqrt(c)
            n = _norm(p)
            return jnp.arctanh(jnp.clip(sc * n, -1.0 + 1e-07, 1.0 - 1e-07)) * p / (sc * n)

        def mobius_add(x, y, c):
            x2 = jnp.sum(x * x, -1, keepdims=True)
            y2 = jnp.sum(y * y, -1, keepdims=True)
            xy = jnp.sum(x * y, -1, keepdims=True)
            num = (1 + 2 * c * xy + c * y2) * x + (1 - c * x2) * y
            den = 1 + 2 * c * xy + c * c * x2 * y2
            return num / jnp.clip(den, MIN_NORM)

        def conv1d(x, w, pad, groups=1):
            return jax.lax.conv_general_dilated(x, w, (1,), [(pad, pad)], dimension_numbers=('NCH', 'OIH', 'NCH'), feature_group_count=groups)

        def batchnorm(x, gamma, beta):
            mean = jnp.mean(x, axis=(0, 2), keepdims=True)
            var = jnp.var(x, axis=(0, 2), keepdims=True)
            xn = (x - mean) * jax.lax.rsqrt(var + 1e-05)
            return gamma[None, :, None] * xn + beta[None, :, None]

        def _reference_tuple_inner(x, w_qkv, bn_gamma, bn_beta, w_dw, w_pw, w_res, b_res):
            c = C_CURV
            h = logmap0(proj(x, c), c)
            h = jnp.transpose(h, (1, 2, 0))
            h = conv1d(h, w_qkv, pad=2)
            h = batchnorm(h, bn_gamma, bn_beta)
            h = jax.nn.relu(jnp.transpose(h, (2, 0, 1)))
            qkv = proj(expmap0(h, c), c)
            t = jnp.transpose(logmap0(proj(qkv, c), c), (1, 2, 0))
            s = conv1d(t, w_dw, pad=2, groups=t.shape[1])
            s = conv1d(s, w_pw, pad=0, groups=t.shape[1] // DIM)
            cat = jnp.concatenate([t, s], axis=1)
            ai = proj(expmap0(jnp.transpose(cat, (2, 0, 1)), c), c)
            t2 = logmap0(proj(ai, c), c)
            L, N, C2 = t2.shape
            g = C2 // (3 * DIM)
            qkv3 = jnp.transpose(t2, (1, 2, 0)).reshape(N, g, 3 * DIM, L)
            q, k, v = jnp.split(qkv3, 3, axis=2)
            q = jax.nn.relu(q)
            k = jax.nn.relu(k)
            vk = jnp.einsum('ngdl,ngel->ngde', v, k)
            out = jnp.einsum('ngde,ngdl->ngdl', vk, q)
            out = out / (jnp.sum(v, -1, keepdims=True) + ATT_EPS)
            out = jnp.transpose(out.reshape(N, g * DIM, L), (2, 0, 1))
            fx_h = proj(expmap0(out, c), c)
            ft = jnp.transpose(logmap0(proj(fx_h, c), c), (1, 2, 0))
            ft = conv1d(ft, w_res, pad=0) + b_res[None, :, None]
            fx = proj(expmap0(jnp.transpose(ft, (2, 0, 1)), c), c)
            residual = mobius_add(fx, x, c)
            return (fx, residual)
        return _reference_tuple_inner(x, w_qkv, bn_gamma, bn_beta, w_dw, w_pw, w_res, b_res)[0]

    def _L0_ffn_ref(x, attention_mask, wr, br, w1, b1, w2, b2):
        import jax, jax.numpy as jnp
        import numpy as np
        B, S, D = (8, 512, 256)
        H = 4 * D
        CAPACITY = 0.5
        b, s, d = x.shape
        weights = (jnp.einsum('bsd,do->bso', x, wr) + br)[..., 0]
        k = max(1, int(CAPACITY * s))
        kk = k - 1 if k > 1 else 1
        _, idx = jax.lax.top_k(weights, k)
        sel_idx = idx[:, :kk]
        sel = jnp.take_along_axis(x, sel_idx[:, :, None], axis=1)
        h = jax.nn.gelu(jnp.einsum('bkd,dh->bkh', sel, w1) + b1)
        y = jnp.einsum('bkh,hd->bkd', h, w2) + b2
        w_sel = jnp.take_along_axis(weights, sel_idx, axis=1)
        y = y * w_sel[..., None]
        batch_idx = jnp.arange(b)[:, None]
        processed = jnp.zeros_like(x).at[batch_idx, sel_idx].set(y)
        return processed + x

    def _L1_gnn_ref(x, edge_index, W0, att_src0, att_dst0, b0, W1, att_src1, att_dst1, b1):
        import jax, jax.numpy as jnp
        import numpy as np
        N = 6250
        E = 100000
        D_IN = 256
        HID = 32
        HEADS = 8
        D_OUT = 64
        NEG_SLOPE = 0.2

        def _gat_conv(x, src, dst, W, att_src, att_dst, bias, heads, out_dim, concat):
            n = x.shape[0]
            h = (x @ W.T).reshape(n, heads, out_dim)
            a_s = jnp.sum(h * att_src, axis=-1)
            a_d = jnp.sum(h * att_dst, axis=-1)
            logits = jax.nn.leaky_relu(a_s[src] + a_d[dst], NEG_SLOPE)
            m = jax.ops.segment_max(logits, dst, num_segments=n)
            e = jnp.exp(logits - m[dst])
            den = jax.ops.segment_sum(e, dst, num_segments=n)
            alpha = e / (den[dst] + 1e-16)
            out = jax.ops.segment_sum(alpha[:, :, None] * h[src], dst, num_segments=n)
            out = out.reshape(n, heads * out_dim) if concat else out.mean(axis=1)
            return out + bias
        n = x.shape[0]
        loop = jnp.arange(n, dtype=edge_index.dtype)
        ei = jnp.concatenate([edge_index, jnp.stack([loop, loop])], axis=1)
        src, dst = (ei[0], ei[1])
        out1 = jax.nn.elu(_gat_conv(x, src, dst, W0, att_src0, att_dst0, b0, HEADS, HID, True))
        _ = _gat_conv(out1, src, dst, W1, att_src1, att_dst1, b1, 1, D_OUT, False)
        return out1

    def _L1_mix_ref(x, Wqkv, bqkv, Wproj, bproj, temperature):
        import jax, jax.numpy as jnp
        import numpy as np
        A, Bc, Cc = (0.5, 1.0, 1.0)
        H = 8
        EPS = 1e-12

        def _normalize(t):
            n = jnp.linalg.norm(t, axis=-1, keepdims=True)
            return t / jnp.maximum(n, EPS)
        B, N, C = x.shape
        D = C // H
        scale = float(D) ** 0.25
        qkv = (x @ Wqkv.T + bqkv).reshape(B, N, 3, H, D)
        qkv = jnp.transpose(qkv, (2, 0, 3, 1, 4))
        q, k, v = (qkv[0], qkv[1], qkv[2])
        q = q * scale
        v1 = jnp.concatenate([jnp.ones((B, H, N, 1), dtype=v.dtype), v], axis=-1)
        qn = _normalize(q) * (scale * temperature)
        kn = _normalize(k) * scale
        vN = v1 / N
        kv_mod = jnp.einsum('bhni,bhnj,bhne->bhije', kn, kn, vN)
        kv = jnp.einsum('bhnd,bhne->bhde', kn, vN)
        vsum = jnp.sum(vN, axis=-2)[:, :, None, :]
        y = A * jnp.einsum('bhni,bhnj,bhije->bhne', qn, qn, kv_mod) + scale ** 2 * Bc * jnp.einsum('bhnd,bhde->bhne', qn, kv) + scale ** 4 * Cc * vsum
        y_norm, y = (y[..., :1], y[..., 1:])
        y = y / y_norm
        out = jnp.transpose(y, (0, 2, 1, 3)).reshape(B, N, H * D)
        return out @ Wproj.T + bproj

    def _L1_ffn_ref(x, W_fx, b_fx, W_x, b_x, W_slice, b_slice, W_q, W_k, W_v, W_out, b_out, temperature):
        import jax, jax.numpy as jnp
        import numpy as np
        DIM = 256
        H = 8
        D = 64
        G = 64
        INNER = H * D
        SCALE = D ** (-0.5)
        B, N, _ = x.shape
        fx_mid = (x @ W_fx + b_fx).reshape(B, N, H, D).transpose(0, 2, 1, 3)
        x_mid = (x @ W_x + b_x).reshape(B, N, H, D).transpose(0, 2, 1, 3)
        temp = jnp.clip(temperature, 0.1, 5.0)
        slice_weights = jax.nn.softmax((x_mid @ W_slice + b_slice) / temp, axis=-1)
        slice_norm = slice_weights.sum(axis=2)
        slice_token = jnp.einsum('bhnc,bhng->bhgc', fx_mid, slice_weights)
        slice_token = slice_token / (slice_norm[..., None] + 1e-05)
        q = slice_token @ W_q
        k = slice_token @ W_k
        v = slice_token @ W_v
        attn = jax.nn.softmax(jnp.einsum('bhgc,bhkc->bhgk', q, k) * SCALE, axis=-1)
        out_slice = jnp.einsum('bhgk,bhkc->bhgc', attn, v)
        out_x = jnp.einsum('bhgc,bhng->bhnc', out_slice, slice_weights)
        out_x = out_x.transpose(0, 2, 1, 3).reshape(B, N, INNER)
        return out_x @ W_out + b_out
    edge_index = jnp.stack([src, dst])
    xn = _layernorm(x, axis=-1)
    x = x + _L0_gnn_ref(xn, edge_index, L0_gnn_Wl1, L0_gnn_bl1, L0_gnn_Wr1, L0_gnn_br1, L0_gnn_att1, L0_gnn_bias1, L0_gnn_Wl2, L0_gnn_bl2, L0_gnn_Wr2, L0_gnn_br2, L0_gnn_att2, L0_gnn_bias2, L0_gnn_Wo, L0_gnn_bo) + _L0_mix_ref(xn[None], L0_mix_w_qkv, L0_mix_bn_gamma, L0_mix_bn_beta, L0_mix_w_dw, L0_mix_w_pw, L0_mix_w_res, L0_mix_b_res)[0]
    x = x + _L0_ffn_ref(_layernorm(x, axis=-1)[None], L0_ffn_attention_mask, L0_ffn_wr, L0_ffn_br, L0_ffn_w1, L0_ffn_b1, L0_ffn_w2, L0_ffn_b2)[0]
    xn = _layernorm(x, axis=-1)
    x = x + _L1_gnn_ref(xn, edge_index, L1_gnn_W0, L1_gnn_att_src0, L1_gnn_att_dst0, L1_gnn_b0, L1_gnn_W1, L1_gnn_att_src1, L1_gnn_att_dst1, L1_gnn_b1) + _L1_mix_ref(xn[None], L1_mix_Wqkv, L1_mix_bqkv, L1_mix_Wproj, L1_mix_bproj, L1_mix_temperature)[0]
    x = x + _L1_ffn_ref(_layernorm(x, axis=-1)[None], L1_ffn_W_fx, L1_ffn_b_fx, L1_ffn_W_x, L1_ffn_b_x, L1_ffn_W_slice, L1_ffn_b_slice, L1_ffn_W_q, L1_ffn_W_k, L1_ffn_W_v, L1_ffn_W_out, L1_ffn_b_out, L1_ffn_temperature)[0]
    return x

_drawn_inputs = setup_inputs


def setup_inputs(seed=0):
    import zlib

    import numpy as np

    out = dict(_drawn_inputs(seed))
    spreads = {'L0_gnn_bl1': (0.0, 0.751),
     'L0_gnn_br1': (0.0, 0.8),
     'L0_gnn_bias1': (0.0, 0.8),
     'L0_gnn_bl2': (0.0, 0.479),
     'L0_gnn_br2': (0.0, 0.8),
     'L0_gnn_bias2': (0.0, 0.525),
     'L0_gnn_bo': (0.0, 0.286),
     'L0_mix_bn_gamma': (1.0, 0.6),
     'L0_mix_bn_beta': (0.0, 0.493),
     'L0_mix_b_res': (0.0, 0.316),
     'L0_ffn_b1': (0.0, 0.8),
     'L0_ffn_b2': (0.0, 0.732),
     'L1_gnn_b0': (0.0, 0.1),
     'L1_gnn_b1': (0.0, 0.1),
     'L1_mix_bqkv': (0.0, 0.498),
     'L1_mix_bproj': (0.0, 0.1),
     'L1_mix_temperature': (1.0, 0.6),
     'L1_ffn_b_fx': (0.0, 0.1),
     'L1_ffn_b_x': (0.0, 0.8),
     'L1_ffn_b_slice': (0.0, 2.0),
     'L1_ffn_b_out': (0.0, 0.343),
     'L1_ffn_temperature': (0.5, 0.6)}
    factors = {'L0_gnn_Wl1': 7.147,
     'L0_gnn_Wr1': 8.0,
     'L0_gnn_att1': 4.11,
     'L0_gnn_Wr2': 8.0,
     'L0_gnn_att2': 8.0,
     'L0_mix_w_dw': 7.104,
     'L0_mix_w_pw': 6.975,
     'L0_ffn_wr': 3.923,
     'L0_ffn_w1': 4.825,
     'L0_ffn_w2': 4.495,
     'L1_mix_Wqkv': 8.0,
     'L1_mix_Wproj': 3.761,
     'L1_ffn_W_x': 8.0,
     'L1_ffn_W_slice': 8.0,
     'L1_ffn_W_q': 8.0,
     'L1_ffn_W_k': 8.0}
    for name, (base, spread) in spreads.items():
        noise = np.random.default_rng([zlib.crc32(name.encode()), seed]).standard_normal(out[name].shape)
        drawn = base * np.exp(spread * noise) if base else spread * noise
        out[name] = jnp.asarray(drawn.astype(out[name].dtype))
    for name, factor in factors.items():
        out[name] = (out[name] * factor).astype(out[name].dtype)
    return out
```

```python
from contextlib import ExitStack
from math import atanh, log

import numpy as np

import concourse.bass as bass
from concourse import mybir

ALU = mybir.AluOpType
ACT = mybir.ActivationFunctionType
AX = mybir.AxisListType
F32 = mybir.dt.float32
I32 = mybir.dt.int32

N, D, E = 6250, 256, 100000
P = 125
NT = N // P
NC = E // P
CB = 8
CP = 100
CK = NC // CP
H0, C0, W0 = 4, 16, 64
H1, C1, W1 = 8, 32, 256
CV = 768
GR, DH = 16, 32
HID = 1024
KEEP = int(0.5 * N) - 1
BIG = 1e38
LN_EPS = 1e-5
MIN_NORM = 1e-15
MAX_NORM = 1.0 - 1e-5
MAX_ATANH = atanh(float(np.float32(MAX_NORM)))
NLE = "natural_log_exp_and_others"


class Chain:

    def __init__(self, eng, sem):
        self.eng, self.sem, self.total, self.base, self.k, self.per = eng, sem, 0, 0, 0, None

    def loop(self, i, per):
        if self.per is None:
            self.total += self.k
        self.base, self.k, self.per = self.total + i * per, 0, per

    def end(self, trips):
        assert self.k == self.per, (self.sem, self.k, self.per)
        self.total += trips * self.per
        self.base, self.k, self.per = self.total, 0, None

    def step(self, ins):
        self.k += 1
        ins.then_inc(self.sem, 1)

    def settle(self):
        self.eng.wait_ge(self.sem, self.base + self.k)

    def link(self, ins):
        self.step(ins)
        self.settle()


class Mem:

    def __init__(self, nc, stack):
        self.nc, self.stack, self.sems = nc, stack, []

    def sb(self, name, shape, dt=F32):
        return self.stack.enter_context(self.nc.sbuf_tensor(name, shape, dt))

    def lasting_sem(self, name):
        return self.nc.alloc_semaphore(name)

    def sem(self, name):
        self.sems.append(self.nc.alloc_semaphore(name))
        return self.sems[-1]

    def gather_sem(self, name):
        return self.nc.alloc_semaphore(name)

    def close_phase(self):
        with self.nc.Block() as block:
            @block.gpsimd
            def _(pool):
                for s in self.sems:
                    pool.sem_clear(s)
        for s in self.sems:
            self.nc.release_semaphore(s)
        self.sems = []

    def dram(self, name, shape, dt=F32):
        return self.nc.dram_tensor(name, shape, dt, kind="Internal").ap()


def phase(build):
    def whole(nc, m, *args, **kw):
        build(nc, m, *args, **kw)
        m.close_phase()
    return whole


def bcast(ap, n):
    return ap.rearrange("(a d) -> a d", a=1).to_broadcast([n, ap.shape[0]])


def rsqrt_act(act, ch, y, v):
    ch.link(act.activation(y, v, ACT.Ln))
    ch.link(act.activation(y, y, ACT.Exp, scale=-0.5))


def rsqrt_refine(dve, ch, y, v, tmp):
    ch.link(dve.tensor_tensor(tmp, y, y, ALU.mult))
    ch.link(dve.tensor_tensor(tmp, tmp, v, ALU.mult))
    ch.link(dve.tensor_scalar(tmp, tmp, -0.5, 1.5, ALU.mult, ALU.add))
    ch.link(dve.tensor_tensor(y, y, tmp, ALU.mult))


DEPTH = 2


def ready(t):
    return t + DEPTH + 1


def free(t):
    return t + 1




@phase
def setup(nc, m, a):
    m.ident = m.sb("ident", [128, 128])
    m.ones = m.sb("ones", [128, 128])
    m.X = m.sb("X", [P, NT, D])
    m.srcT = m.sb("srcT", [P, NC], I32)
    m.dstT = m.sb("dstT", [P, NC])
    m.mean = m.sb("mean", [P, NT])
    m.rstd = m.sb("rstd", [P, NT])
    m.var = m.sb("var", [P, NT])
    m.start_i = m.sb("start_i", [P, NT], I32)
    m.slot_i = m.sb("slot_i", [P, NT], I32)
    m.next_i = m.sb("next_i", [P, NT], I32)
    m.has = m.sb("has", [P, NT])
    m.gate1 = m.sb("gate1", [P, NT])
    m.gate2 = m.sb("gate2", [P, NT])
    m.df_i = m.sb("df_i", [CP, CK], I32)
    m.seg_col = m.sb("seg_col", [CP, CK])
    m.seg_row = m.sb("seg_row", [CP, NC])
    m.s_const = m.lasting_sem("s_const")
    m.s_pass = m.lasting_sem("s_pass")
    m.s_x = m.lasting_sem("s_x")
    m.starts = m.dram("starts", (N + 1, 1), I32)
    m.edge_rows = m.dram("edge_rows", (E, W0))
    m.edge_rows8 = m.dram("edge_rows8", (E, H1))
    m.pieces0 = m.dram("pieces0", (E, W0 + 2 * H0))
    m.pieces1 = m.dram("pieces1", (E, W1 + 2 * H1))
    m.tl = m.dram("tl", (N, W0))
    m.tr = m.dram("tr", (N, W0))
    m.th = m.dram("th", (N, W1 + H1))
    m.td = m.dram("td", (N, H1))
    m.rest0 = m.dram("rest0", (NC, W0 + 2 * H0))
    m.rest1 = m.dram("rest1", (NC, W1 + 2 * H1))
    m.s_zero = m.lasting_sem("s_zero")
    s_ld, s_ldc, s_io, s_mk = m.sem("ix_ld"), m.sem("ix_ldc"), m.sem("ix_io"), m.sem("ix_mk")
    s_q, s_cmp, s_st, s_ii = m.sem("ix_q"), m.sem("ix_cmp"), m.sem("ix_st"), m.sem("ix_ii")
    c_dve, c_pool, s_d12, s_rel = m.sem("ix_dve"), m.sem("ix_pool"), m.sem("ix_d12"), m.sem("ix_rel")
    with ExitStack() as st:
        def sb(name, shape, dt=F32):
            return st.enter_context(nc.sbuf_tensor(name, shape, dt))
        dsti = sb("dsti", [P, NC], I32)
        dstTi = sb("dstTi", [P, NC], I32)
        dst2 = sb("dst2", [P, NC])
        rn_i = sb("rn_i", [P, 1], I32)
        rn = sb("rn", [P, 1])
        r0 = sb("r0", [P, NT])
        r1 = sb("r1", [P, NT])
        tstep = sb("tstep", [P, NT])
        nio = sb("nio", [P, P])
        ncol = sb("ncol", [P, NT])
        d12 = [sb(f"d12{b}", [P, 2, P]) for b in range(2)]
        sel = [sb(f"sel{b}", [P, P]) for b in range(2)]
        below = sb("below", [P, 2, 2, NC // 2])
        cnt = sb("cnt", [P, NT])
        nrows = sb("nrows", [P, NT])
        es = sb("es", [P, NT])
        es1_i = sb("es1_i", [P, NT], I32)
        es1 = sb("es1", [P, NT])
        tmp = sb("tmp", [P, NT])
        jf = sb("jf", [P, NT])
        last = sb("last", [1, 1], I32)
        dfr_i = sb("dfr_i", [CP, NC], I32)
        pvr_i = sb("pvr_i", [CP, NC], I32)
        dfr = sb("dfr", [CP, NC])
        pvr = sb("pvr", [CP, NC])
        own = sb("own", [CP, NC])
        pvc_i = sb("pvc_i", [CP, CK], I32)
        pvc = sb("pvc", [CP, CK])
        dfc = sb("dfc", [CP, CK])
        ownc = sb("ownc", [CP, CK])
        zero = sb("zero", [P, 2048])
        ps_cnt = [st.enter_context(nc.psum_tensor(f"ps_cnt{b}", [P, 2, 512], F32)) for b in range(2)]
        ps_q = [st.enter_context(nc.psum_tensor(f"ps_q{b}", [P, 512], F32)) for b in range(2)]
        block = st.enter_context(nc.Block())
        xv = a["x"].rearrange("(t p) d -> p t d", p=P)

        @block.sync
        def _(sp):
            sp.dma_start(dsti[:], a["dst"].rearrange("(p j) -> p j", p=P)).then_inc(s_ld, 16)
            sp.dma_start(dstTi[:], a["dstT"]).then_inc(s_ld, 16)
            sp.dma_start(m.srcT[:], a["srcT"]).then_inc(s_ld, 16)
            sp.wait_ge(s_mk, 1)
            with nc.allow_non_contiguous_dma(reason="a column of indices"):
                sp.dma_start(rn_i[0:P - 1, :], a["dst"].rearrange("(p j) -> p j", p=P)[1:P, 0:1]).then_inc(s_ld, 16)
                sp.dma_start(m.df_i[:], a["dstT"][0].rearrange("(k p) -> p k", p=CP)).then_inc(s_ldc, 16)
                sp.dma_start(pvc_i[:, 1:CK], a["dstT"][P - 1, CP - 1:NC - 1].rearrange("(k p) -> p k", p=CP)
                             ).then_inc(s_ldc, 16)
                sp.dma_start(pvc_i[1:CP, 0:1], a["dstT"][P - 1, 0:CP - 1].rearrange("(p a) -> p a", a=1)
                             ).then_inc(s_ldc, 16)
            sp.dma_start(dfr_i[:], bcast(a["dstT"][0], CP)).then_inc(s_ldc, 16)
            sp.dma_start(pvr_i[:, 1:NC], bcast(a["dstT"][P - 1, 0:NC - 1], CP)).then_inc(s_ldc, 16)
            sp.dma_start(m.X[:], xv).then_inc(m.s_x, 16)
            sp.wait_ge(s_st, 1)
            with nc.allow_non_contiguous_dma(reason="a column of indices"):
                sp.dma_start(m.starts[0:N].rearrange("(t p) a -> p (t a)", p=P), m.start_i[:]).then_inc(s_ii, 16)
                sp.dma_start(m.starts[N:N + 1], last[:]).then_inc(s_ii, 16)
                sp.wait_ge(s_ii, 32)
                sp.dma_start(es1_i[:], m.starts[1:N + 1].rearrange("(t p) a -> p (t a)", p=P)).then_inc(s_ii, 16)

        @block.scalar
        def _(act):
            act.wait_ge(s_mk, 2)
            rows = m.edge_rows.rearrange("(p r) w -> p (r w)", p=P)
            for j in range(E * W0 // P // 2048):
                act.dma_start(rows[:, j * 2048:(j + 1) * 2048], zero[:]).then_inc(m.s_zero, 16)
            rows8 = m.edge_rows8.rearrange("(p r) w -> p (r w)", p=P)
            for j in range(0, E * H1 // P, 1600):
                act.dma_start(rows8[:, j:j + 1600], zero[:, 0:1600]).then_inc(m.s_zero, 16)

        @block.gpsimd
        def _(pool):
            ch = Chain(pool, c_pool)
            ch.link(pool.memset(m.ident[:], 0.0))
            pool.memset(m.ones[:], 1.0).then_inc(m.s_const, 1)
            pool.affine_select(out=m.ident[:], in_=m.ident[:], compare_op=ALU.not_equal, fill=1.0, base=0,
                               pattern=[[-1, 128]], channel_multiplier=1).then_inc(m.s_const, 1)
            pool.iota(nio[:], pattern=[[1, P]], base=0, channel_multiplier=0,
                      allow_small_or_imprecise_dtypes=True).then_inc(s_io, 1)
            pool.iota(ncol[:], pattern=[[P, NT]], base=0, channel_multiplier=1,
                      allow_small_or_imprecise_dtypes=True).then_inc(s_io, 1)
            pool.iota(tstep[:], pattern=[[P, NT]], base=0, channel_multiplier=0,
                      allow_small_or_imprecise_dtypes=True).then_inc(s_io, 1)
            pool.iota(own[:], pattern=[[1, NC]], base=1, channel_multiplier=0,
                      allow_small_or_imprecise_dtypes=True).then_inc(s_io, 1)
            pool.iota(ownc[:], pattern=[[CP, CK]], base=1, channel_multiplier=1,
                      allow_small_or_imprecise_dtypes=True).then_inc(s_io, 1)

        @block.vector
        def _(dve):
            ch = Chain(dve, c_dve)
            dve.memset(last[:], E)
            dve.memset(pvr_i[:, 0:1], -1)
            dve.memset(pvc_i[:], -1)
            ch.link(dve.memset(rn_i[:], 2 * N))
            dve.memset(zero[:], 0.0).then_inc(s_mk, 1)
            dve.wait_ge(s_mk, 1)
            dve.engine_nop().then_inc(s_mk, 1)
            dve.wait_ge(s_ld, 64)
            ch.link(dve.tensor_copy(dst2[:], dsti[:]))
            ch.link(dve.tensor_copy(m.dstT[:], dstTi[:]))
            ch.link(dve.tensor_copy(rn[:], rn_i[:]))
            dve.wait_ge(s_io, 5)
            ch.step(dve.tensor_scalar(r0[:], tstep[:], -1.0, dst2[:, 0:1], ALU.mult, ALU.add))
            ch.link(dve.tensor_scalar(r1[:], tstep[:], -1.0, rn[:, 0:1], ALU.mult, ALU.add))
            dve.sem_inc(s_cmp, 2 * DEPTH)

            def select(t, b):
                dve.wait_ge(s_q, free(t))
                ch.step(dve.tensor_scalar(d12[b][:, 0, :], nio[:], r0[:, bass.ds(t, 1)], None, ALU.is_gt))
                ch.link(dve.tensor_scalar(d12[b][:, 1, :], nio[:], r1[:, bass.ds(t, 1)], None, ALU.is_gt))
                dve.tensor_tensor(sel[b][:], d12[b][:, 0, :], d12[b][:, 1, :], ALU.subtract).then_inc(s_d12, 1)

            def count(t, b):
                dve.wait_ge(s_q, ready(t))
                dve.tensor_scalar(below[:, b], ps_cnt[b][:, :, 0:NC // 2], ncol[:, bass.ds(t, 1)], None, ALU.is_lt,
                                  ALU.add, accum_out=cnt[:, bass.ds(t, 1)]).then_inc(s_cmp, 1)
                dve.tensor_copy(nrows[:, bass.ds(t, 1)], ps_q[b][:, 0:1]).then_inc(s_cmp, 1)
            select(0, 0)
            with dve.Fori(0, NT // 2 - 1) as i:
                ch.loop(i, 4)
                select(2 * i + 1, 1)
                count(2 * i, 0)
                select(2 * i + 2, 0)
                count(2 * i + 1, 1)
            ch.end(NT // 2 - 1)
            select(NT - 1, 1)
            count(NT - 2, 0)
            count(NT - 1, 1)
            dve.wait_ge(s_cmp, 2 * NT + 2 * DEPTH)
            ch.link(dve.tensor_scalar(tmp[:], nrows[:], float(NC), -float(NC), ALU.mult, ALU.add))
            ch.link(dve.tensor_tensor(tmp[:], tmp[:], cnt[:], ALU.add))
            ch.link(dve.tensor_scalar(es[:], tmp[:], 0.0, None, ALU.max))
            dve.tensor_copy(m.start_i[:], es[:]).then_inc(s_st, 1)
            dve.wait_ge(s_ii, 48)
            ch.link(dve.tensor_copy(es1[:], es1_i[:]))
            ch.link(dve.tensor_tensor(m.has[:], es1[:], es[:], ALU.is_gt))
            ch.step(dve.tensor_scalar(m.gate1[:], m.has[:], 2 * BIG, -BIG, ALU.mult, ALU.add))
            ch.link(dve.tensor_scalar(tmp[:], m.has[:], -2.0 * E, 2.0 * E, ALU.mult, ALU.add))
            ch.link(dve.tensor_tensor(tmp[:], tmp[:], es[:], ALU.add))
            ch.link(dve.tensor_copy(m.slot_i[:], tmp[:]))
            ch.link(dve.tensor_scalar(tmp[:], es[:], 1.0 / P, 0.5 / P - 0.5, ALU.mult, ALU.add))
            ch.link(dve.tensor_copy(m.next_i[:], tmp[:]))
            ch.link(dve.tensor_copy(jf[:], m.next_i[:]))
            ch.link(dve.tensor_scalar(jf[:], jf[:], 1.0, None, ALU.add))
            ch.link(dve.tensor_scalar(tmp[:], jf[:], float(P), None, ALU.mult))
            ch.link(dve.tensor_tensor(tmp[:], es1[:], tmp[:], ALU.is_gt))
            ch.link(dve.tensor_scalar(m.gate2[:], tmp[:], 2 * BIG, -BIG, ALU.mult, ALU.add))
            ch.link(dve.tensor_scalar(jf[:], jf[:], NC - 1.0, None, ALU.min))
            ch.link(dve.tensor_copy(m.next_i[:], jf[:]))
            ch.link(dve.tensor_scalar(es[:], es[:], E - 1.0, None, ALU.min))
            ch.link(dve.tensor_copy(m.start_i[:], es[:]))
            dve.wait_ge(s_ldc, 80)
            for seg, di, pi, dd, pp, oo in ((m.seg_row, dfr_i, pvr_i, dfr, pvr, own),
                                            (m.seg_col, m.df_i, pvc_i, dfc, pvc, ownc)):
                ch.link(dve.tensor_copy(dd[:], di[:]))
                ch.link(dve.tensor_copy(pp[:], pi[:]))
                ch.link(dve.tensor_tensor(pp[:], dd[:], pp[:], ALU.is_equal))
                ch.link(dve.tensor_tensor(dd[:], dd[:], oo[:], ALU.add))
                ch.link(dve.tensor_tensor(dd[:], dd[:], pp[:], ALU.mult))
                ch.link(dve.tensor_tensor(seg[:], dd[:], oo[:], ALU.subtract))

        @block.tensor
        def _(pe):
            pe.wait_ge(m.s_const, 2)
            pe.sem_inc(s_q, DEPTH)
            with pe.Fori(0, NT // 2) as i:
                for b in range(2):
                    t = 2 * i + b
                    pe.wait_ge(s_d12, t + 1)
                    pe.wait_ge(s_cmp, 2 * free(t))
                    pe.sem_inc(m.s_pass, 1)
                    for j in range(2):
                        pe.matmul(ps_cnt[b][:, j, 0:NC // 2], sel[b][:], dst2[:, j * (NC // 2):(j + 1) * (NC // 2)],
                                  start=True, stop=True)
                    pe.matmul(ps_q[b][:, 0:1], d12[b][:, 0, :], m.ones[0:P, 0:1], start=True, stop=True
                              ).then_inc(s_q, 1)




@phase
def norm_stats(nc, m, tag, ball=False):
    s_sum, s_v, s_y, s_z, s_l = (m.sem(f"{tag}_{n}") for n in ("sum", "v", "y", "z", "l"))
    c_dve, c_act = m.sem(f"{tag}_dve"), m.sem(f"{tag}_act")
    with ExitStack() as st:
        def sb(name, shape, dt=F32):
            return st.enter_context(nc.sbuf_tensor(f"{tag}_{name}", shape, dt))
        st6 = sb("st6", [P, NT, 6])
        ve, tmp, n2, y, lo, hi, msk, nn = (sb(n, [P, NT]) for n in ("ve", "tmp", "n2", "y", "lo", "hi", "msk", "nn"))
        block = st.enter_context(nc.Block())

        @block.vector
        def _(dve):
            ch = Chain(dve, c_dve)
            dve.wait_ge(m.s_x, 16)
            with dve.Fori(0, NT // 10) as i:
                ch.loop(i, 10)
                for j in range(10):
                    ch.step(dve.bn_stats(st6[:, 10 * i + j, :], m.X[:, 10 * i + j, :]))
            ch.end(NT // 10)
            ch.settle()
            ch.step(dve.tensor_tensor(m.mean[:], st6[:, :, 1], st6[:, :, 4], ALU.add))
            ch.step(dve.tensor_tensor(tmp[:], st6[:, :, 1], st6[:, :, 4], ALU.subtract))
            ch.link(dve.tensor_tensor(m.var[:], st6[:, :, 2], st6[:, :, 5], ALU.add))
            ch.step(dve.tensor_scalar(m.mean[:], m.mean[:], 0.5, None, ALU.mult))
            ch.step(dve.tensor_tensor(tmp[:], tmp[:], tmp[:], ALU.mult))
            ch.link(dve.tensor_scalar(m.var[:], m.var[:], 1.0 / D, None, ALU.mult))
            ch.link(dve.scalar_tensor_tensor(m.var[:], tmp[:], 0.25, m.var[:], ALU.mult, ALU.add))
            dve.tensor_scalar(ve[:], m.var[:], LN_EPS, None, ALU.add).then_inc(s_v, 1)
            dve.wait_ge(s_y, 1)
            dve.wait_ge(s_v, 1)
            rsqrt_refine(dve, ch, m.rstd[:], ve[:], tmp[:])
            if not ball:
                return
            ch.link(dve.tensor_tensor(n2[:], m.rstd[:], m.rstd[:], ALU.mult))
            ch.link(dve.tensor_tensor(n2[:], n2[:], m.var[:], ALU.mult))
            dve.tensor_scalar(n2[:], n2[:], float(D), MIN_NORM ** 2, ALU.mult, ALU.max).then_inc(s_v, 1)
            dve.wait_ge(s_y, 2)
            dve.wait_ge(s_v, 2)
            rsqrt_refine(dve, ch, y[:], n2[:], tmp[:])
            ch.link(dve.tensor_tensor(nn[:], n2[:], y[:], ALU.mult))
            ch.link(dve.tensor_scalar(nn[:], nn[:], MAX_NORM, None, ALU.min))
            ch.link(dve.tensor_scalar(lo[:], nn[:], -1.0, 1.0, ALU.mult, ALU.add))
            dve.tensor_scalar(hi[:], nn[:], 1.0, None, ALU.add).then_inc(s_v, 1)
            ch.link(dve.tensor_tensor(tmp[:], nn[:], nn[:], ALU.mult))
            ch.link(dve.tensor_scalar(n2[:], tmp[:], 1.0 / 11, 1.0 / 9, ALU.mult, ALU.add))
            for c in (1.0 / 7, 1.0 / 5, 1.0 / 3, 1.0):
                ch.link(dve.tensor_tensor(n2[:], n2[:], tmp[:], ALU.mult))
                ch.link(dve.tensor_scalar(n2[:], n2[:], c, None, ALU.add))
            ch.link(dve.tensor_scalar(msk[:], nn[:], 0.2, None, ALU.is_lt))
            ch.link(dve.tensor_tensor(n2[:], n2[:], msk[:], ALU.mult))
            dve.wait_ge(s_l, 2)
            ch.link(dve.tensor_tensor(hi[:], hi[:], lo[:], ALU.subtract))
            ch.link(dve.scalar_tensor_tensor(hi[:], hi[:], 0.5, y[:], ALU.mult, ALU.mult))
            ch.link(dve.tensor_scalar(msk[:], msk[:], -1.0, 1.0, ALU.mult, ALU.add))
            ch.link(dve.tensor_tensor(hi[:], hi[:], msk[:], ALU.mult))
            ch.link(dve.tensor_tensor(m.fac[:], hi[:], n2[:], ALU.add))
            ch.link(dve.tensor_tensor(m.rfac[:], m.fac[:], m.rstd[:], ALU.mult))

        @block.scalar
        def _(act):
            ch = Chain(act, c_act)
            act.preload_act_table_set(NLE)
            act.wait_ge(s_v, 1)
            ch.link(act.activation(m.rstd[:], ve[:], ACT.Ln))
            act.activation(m.rstd[:], m.rstd[:], ACT.Exp, scale=-0.5).then_inc(s_y, 1)
            if ball:
                act.wait_ge(s_v, 2)
                ch.link(act.activation(y[:], n2[:], ACT.Ln))
                act.activation(y[:], y[:], ACT.Exp, scale=-0.5).then_inc(s_y, 1)
                act.wait_ge(s_v, 3)
                act.activation(lo[:], lo[:], ACT.Ln).then_inc(s_l, 1)
                act.activation(hi[:], hi[:], ACT.Ln).then_inc(s_l, 1)




@phase
def node_tables(nc, m, tag, w, cols, split, gathered, spread, slots, bias=None, gram=None):
    s_xn, s_xT, s_pT, s_w, s_tab, s_a, s_g, s_ix, s_z, s_gs = (
        m.sem(f"{tag}_{n}") for n in ("xn", "xT", "pT", "w", "tab", "a", "g", "ix", "z", "gs"))
    s_o = [m.sem(f"{tag}_o{b}") for b in range(2)]
    s_sc = [m.gather_sem(f"{tag}_sc{b}") for b in range(2)]
    c_pool = m.sem(f"{tag}_pool")
    tail = cols - split
    with ExitStack() as st:
        def sb(name, shape, dt=F32):
            return st.enter_context(nc.sbuf_tensor(f"{tag}_{name}", shape, dt))
        xn = sb("xn", [P, 2, D])
        xT = sb("xT", [128, 2, 2, P])
        tab = sb("tab", [P, 2, split])
        own = [sb(f"own{b}", [P, tail]) for b in range(2)]
        slot = [sb(f"slot{b}", [P, 1], I32) for b in range(2)]
        am = sb("am", [P, 2, D + 2])
        zero = sb("zero", [P, 512])
        ps_t = [st.enter_context(nc.psum_tensor(f"{tag}_pt{b}", [128, 2, P], F32)) for b in range(2)]
        ps_w = [st.enter_context(nc.psum_tensor(f"{tag}_pw{b}", [P, 512], F32)) for b in range(2)]
        ps_g = [st.enter_context(nc.psum_tensor(f"{tag}_pg{b}", [128, 512], F32)) for b in range(2)]
        block = st.enter_context(nc.Block())
        gath_v = gathered.rearrange("(t p) w -> t p w", p=P)
        spre_v = spread.rearrange("(t p) w -> t p w", p=P)

        @block.vector
        def _(dve):
            dve.sem_inc(s_xn, DEPTH)
            dve.sem_inc(s_tab, 2 * DEPTH)
            if gram is not None:
                dve.memset(zero[:], 0.0).then_inc(s_z, 1)
                dve.memset(am[:, :, D:D + 2], 1.0).then_inc(s_z, 1)
            with dve.Fori(0, NT // 2) as i:
                for b in range(2):
                    t = 2 * i + b
                    dve.wait_ge(s_pT, free(t))
                    if gram is not None:
                        dve.wait_ge(s_a, free(t))
                    dve.tensor_scalar(xn[:, b, :], m.X[:, t, :], m.mean[:, bass.ds(t, 1)], m.rstd[:, bass.ds(t, 1)],
                                      ALU.subtract, ALU.mult).then_inc(s_xn, 1)
                for b in range(2):
                    t = 2 * i + b
                    dve.wait_ge(s_sc[b], 16 * i)
                    dve.tensor_copy(slot[b][:], m.slot_i[:, bass.ds(t, 1)]).then_inc(s_ix, 1)
                    dve.wait_ge(s_o[b], 32 * i)
                    dve.wait_ge(s_w, ready(t))
                    for lo, hi, dst in ((0, split, tab[:, b, :]), (split, cols, own[b][:])):
                        if bias is None:
                            dve.tensor_copy(dst, ps_w[b][:, lo:hi]).then_inc(s_tab, 1)
                        else:
                            dve.tensor_tensor(dst, ps_w[b][:, lo:hi], bias[:, lo:hi], ALU.add).then_inc(s_tab, 1)

        @block.scalar
        def _(act):
            act.sem_inc(s_xT, DEPTH)
            act.sem_inc(s_a, DEPTH)
            act.wait_ge(m.s_const, 2)
            with act.Fori(0, NT // 2) as i:
                for b in range(2):
                    t = 2 * i + b
                    act.wait_ge(s_w, free(t))
                    act.wait_ge(s_pT, ready(t))
                    act.activation(xT[:, b], ps_t[b][:], ACT.Copy).then_inc(s_xT, 1)
                for b in range(2):
                    t = 2 * i + b
                    if gram is not None:
                        act.wait_ge(s_g, free(t))
                        act.wait_ge(s_z, 2)
                        act.activation(am[:, b, 0:D], xn[:, b, :], ACT.Copy,
                                       scale=m.fac[:, bass.ds(t, 1)]).then_inc(s_a, 1)
            if gram is not None:
                act.wait_ge(s_g, DEPTH + NT + 1)
                for k in range(2):
                    act.activation(gram[:, k, :], ps_g[k][:, 0:D + 1], ACT.Copy).then_inc(s_gs, 1)

        @block.tensor
        def _(pe):
            pe.sem_inc(s_w, DEPTH)
            pe.sem_inc(s_pT, DEPTH)
            pe.sem_inc(s_g, DEPTH)
            pe.wait_ge(m.s_const, 2)
            if gram is not None:
                pe.wait_ge(s_z, 2)
                for k in range(2):
                    pe.matmul(ps_g[k][:, 0:D + 1], zero[:, 0:128], zero[:, 0:D + 1], start=True, stop=False,
                              skip_group_check=True)
            with pe.Fori(0, NT // 2) as i:
                for b in range(2):
                    t = 2 * i + b
                    pe.wait_ge(s_xT, free(t))
                    pe.wait_ge(s_xn, ready(t))
                    for k in range(2):
                        mm = pe.transpose(ps_t[b][:, k, :], xn[:, b, k * 128:(k + 1) * 128], m.ident[0:P, 0:P])
                    mm.then_inc(s_pT, 1)
                for b in range(2):
                    t = 2 * i + b
                    pe.wait_ge(s_tab, 2 * free(t))
                    pe.wait_ge(s_xT, ready(t))
                    for k in range(2):
                        mm = pe.matmul(ps_w[b][:, 0:cols], xT[:, b, k, :], w[:, k, 0:cols], start=(k == 0),
                                       stop=(k == 1))
                    mm.then_inc(s_w, 1)
                    if gram is not None:
                        pe.wait_ge(s_a, ready(t))
                        for k in range(2):
                            mm = pe.matmul(ps_g[k][:, 0:D + 1], am[:, b, k * 128:(k + 1) * 128], am[:, b, 0:D + 1],
                                           start=False, stop=False, skip_group_check=True)
                        mm.then_inc(s_g, 1)
            if gram is not None:
                for k in range(2):
                    mm = pe.matmul(ps_g[k][:, 0:D + 1], zero[:, 0:128], zero[:, 0:D + 1], start=False, stop=True,
                                   skip_group_check=True)
                mm.then_inc(s_g, 1)

        @block.sync
        def _(sp):
            with sp.Fori(0, NT // 2) as i:
                for b in range(2):
                    t = 2 * i + b
                    sp.wait_ge(s_tab, 2 * ready(t))
                    sp.dma_start(gath_v[t], tab[:, b, :]).then_inc(s_o[b], 16)
                    sp.dma_start(spre_v[t], own[b][:]).then_inc(s_o[b], 16)
            for b in range(2):
                sp.wait_ge(s_o[b], 16 * NT)

        @block.gpsimd
        def _(pool):
            pool.wait_ge(m.s_zero, 464)
            limit = pool.to_reg(E - 1)
            with pool.Fori(0, NT // 2) as i:
                for b in range(2):
                    t = 2 * i + b
                    pool.wait_ge(s_tab, 2 * ready(t))
                    pool.wait_ge(s_ix, t + 1)
                    pool.sem_inc(m.s_pass, 1)
                    pool.indirect_dma_start(out=slots, out_offset=bass.IndirectOffsetOnAxis(ap=slot[b][:], axis=0),
                                            in_=own[b][:], in_offset=None, bounds_check=limit,
                                            oob_is_err=False).then_inc(s_sc[b], 16)
            for b in range(2):
                pool.wait_ge(s_sc[b], 16 * NT // 2)



@phase
def fold_batch_norm(nc, m, wc, bnb, gram, gamma, beta):
    s_mu, s_s, s_gw, s_e, s_pr, s_v, s_y = (m.sem(f"bn_{n}") for n in ("mu", "s", "gw", "e", "pr", "v", "y"))
    c_dve, c_act = m.sem("bn_dve"), m.sem("bn_act")
    HV = CV // 2
    with ExitStack() as st:
        def sb(name, shape, dt=F32):
            return st.enter_context(nc.sbuf_tensor(f"bn_{name}", shape, dt))
        mub = sb("mub", [128, 2, 128])
        prod = sb("prod", [128, 2, CV])
        mean, var, y, tmp = (sb(n, [128, CV]) for n in ("mean", "var", "y", "tmp"))
        ps_m = st.enter_context(nc.psum_tensor("bn_pm", [128, 2, 512], F32))
        ps_e = st.enter_context(nc.psum_tensor("bn_pe", [128, 2, 512], F32))
        ps_w = st.enter_context(nc.psum_tensor("bn_pw", [128, 4, 512], F32))
        block = st.enter_context(nc.Block())

        def halves(t):
            return t.rearrange("p (j n) -> p j n", j=2)

        @block.tensor
        def _(pe):
            pe.wait_ge(s_mu, 2)
            for j in range(2):
                for k in range(2):
                    mm = pe.matmul(ps_m[:, j, 0:HV], mub[:, k, :], wc[:, k, j * HV:(j + 1) * HV],
                                   start=(k == 0), stop=(k == 1))
            mm.then_inc(s_s, 1)
            for k1 in range(2):
                for j in range(2):
                    for k in range(2):
                        mm = pe.matmul(ps_w[:, 2 * k1 + j, 0:HV], gram[:, k, k1 * 128:(k1 + 1) * 128],
                                       wc[:, k, j * HV:(j + 1) * HV], start=(k == 0), stop=(k == 1))
            mm.then_inc(s_gw, 1)
            pe.wait_ge(s_pr, 2)
            for j in range(2):
                for k in range(2):
                    mm = pe.matmul(ps_e[:, j, 0:HV], m.ones[:], prod[:, k, j * HV:(j + 1) * HV],
                                   start=(k == 0), stop=(k == 1))
            mm.then_inc(s_e, 1)

        @block.vector
        def _(dve):
            ch = Chain(dve, c_dve)
            for k in range(2):
                dve.tensor_scalar(mub[:, k, :], m.ones[:], gram[:, k, D:D + 1], None, ALU.mult).then_inc(s_mu, 1)
            dve.wait_ge(s_gw, 1)
            for k in range(2):
                dve.tensor_tensor(halves(prod[:, k, :]), ps_w[:, 2 * k:2 * k + 2, 0:HV], halves(wc[:, k, :]),
                                  ALU.mult).then_inc(s_pr, 1)
            dve.wait_ge(s_s, 1)
            ch.link(dve.tensor_scalar(halves(mean[:]), ps_m[:, :, 0:HV], 1.0 / N, None, ALU.mult))
            ch.link(dve.tensor_tensor(tmp[:], mean[:], mean[:], ALU.mult))
            dve.wait_ge(s_e, 1)
            ch.link(dve.scalar_tensor_tensor(halves(var[:]), ps_e[:, :, 0:HV], 1.0 / N, halves(tmp[:]),
                                             ALU.mult, ALU.subtract))
            dve.tensor_scalar(var[:], var[:], 0.0, LN_EPS, ALU.max, ALU.add).then_inc(s_v, 1)
            dve.wait_ge(s_y, 1)
            dve.wait_ge(s_v, 1)
            rsqrt_refine(dve, ch, y[:], var[:], tmp[:])
            ch.link(dve.tensor_tensor(y[:], y[:], gamma[:], ALU.mult))
            ch.step(dve.tensor_tensor(wc[:, 0, :], wc[:, 0, :], y[:], ALU.mult))
            ch.step(dve.tensor_tensor(wc[:, 1, :], wc[:, 1, :], y[:], ALU.mult))
            ch.link(dve.tensor_tensor(mean[:], mean[:], y[:], ALU.mult))
            ch.link(dve.tensor_tensor(bnb[:], beta[0:P, :], mean[0:P, :], ALU.subtract))

        @block.scalar
        def _(act):
            ch = Chain(act, c_act)
            act.preload_act_table_set(NLE)
            act.wait_ge(s_v, 1)
            ch.link(act.activation(y[:], var[:], ACT.Ln))
            act.activation(y[:], y[:], ACT.Exp, scale=-0.5).then_inc(s_y, 1)




class Mixer:

    def __init__(self, nc, m, st, wc, bnb, blockdiag, res, b_res):
        def sb(name, shape, dt=F32):
            return st.enter_context(nc.sbuf_tensor(f"mx_{name}", shape, dt))
        self.nc, self.m, self.wc, self.bnb, self.bd, self.res, self.b_res = nc, m, wc, bnb, blockdiag, res, b_res
        self.a = sb("a", [P, D])
        self.aT = sb("aT", [128, 2, P])
        self.hb = sb("hb", [P, CV])
        self.cat = sb("cat", [P, 2 * CV])
        self.junk = sb("junk", [P, 2 * CV])
        self.tT = sb("tT", [128, 6, P])
        self.vs, self.num, self.kr, self.den, self.o = (sb(n, [P, GR, DH]) for n in ("vs", "num", "kr", "den", "o"))
        self.sk = sb("sk", [P, GR])
        self.oT = sb("oT", [128, 4, P])
        self.ft = sb("ft", [P, D])
        self.n2, self.ln, self.nn, self.f = (sb(n, [P, 4]) for n in ("n2", "ln", "nn", "f"))
        self.rn, self.e2, self.e3 = sb("rn", [P, 1]), sb("e2", [P, 2]), sb("e3", [P, 1])
        self.tiny, self.lnmax = sb("tiny", [P, 1]), sb("lnmax", [P, 1])
        self.s_a, self.s_pa, self.s_aT, self.s_h, self.s_hb, self.s_nr, self.s_f, self.s_t, self.s_pt = (
            m.lasting_sem("mx_" + n) for n in ("a", "pa", "aT", "h", "hb", "nr", "f", "t", "pt"))
        self.s_tT, self.s_s, self.s_o, self.s_po, self.s_oT, self.s_r, self.s_ft, self.s_out = (
            m.lasting_sem("mx_" + n) for n in ("tT", "s", "o", "po", "oT", "r", "ft", "out"))

    def banks(self, st, tag):
        self.ps_t = st.enter_context(self.nc.psum_tensor(f"{tag}_mx_pt", [128, 2, 512], F32))
        self.ps_h = st.enter_context(self.nc.psum_tensor(f"{tag}_mx_ph", [P, 2, 512], F32))

    DVE_STEPS = 13

    def dve(self, dve, ch, t, stage):
        m = self.m
        if stage == 0:
            dve.tensor_scalar(self.a[:], m.X[:, t, :], m.mean[:, bass.ds(t, 1)], m.rfac[:, bass.ds(t, 1)],
                              ALU.subtract, ALU.mult).then_inc(self.s_a, 1)
        elif stage == 1:
            dve.wait_ge(self.s_h, t + 1)
            dve.tensor_tensor(self.hb.rearrange("p (j n) -> p j n", j=2), self.ps_h[:, :, 0:CV // 2],
                              self.bnb.rearrange("p (j n) -> p j n", j=2), ALU.add).then_inc(self.s_hb, 1)
        elif stage == 2:
            dve.wait_ge(self.s_f, 3 * t + 2)
            q, k, v = (self.cat.rearrange("p (g c d) -> p g c d", g=GR, c=3)[:, :, c, :] for c in range(3))
            f2 = self.f[:, 1:2]
            ch.step(dve.tensor_scalar(self.vs[:], v, f2, None, ALU.mult))
            ch.step(dve.tensor_scalar(self.kr[:], k, 0.0, f2, ALU.max, ALU.mult))
            ch.link(dve.tensor_scalar(self.den[:], v, f2, MIN_NORM, ALU.mult, ALU.add))
            ch.step(dve.scalar_tensor_tensor(self.num[:], q, 0.0, self.vs[:], ALU.max, ALU.mult))
            ch.step(dve.reciprocal(self.den[:], self.den[:]))
            ch.link(dve.tensor_reduce(self.sk[:], self.kr[:], AX.X, ALU.add))
            ch.step(dve.tensor_scalar(self.sk[:], self.sk[:], f2, None, ALU.mult))
            ch.link(dve.tensor_tensor(self.num[:], self.num[:], self.den[:], ALU.mult))
            dve.tensor_tensor(self.o[:], self.num[:], self.sk[:].unsqueeze(2).to_broadcast([P, GR, DH]), ALU.mult
                              ).then_inc(self.s_o, 1)
        elif stage == 3:
            dve.wait_ge(self.s_f, 3 * t + 3)
            dve.wait_ge(self.s_r, t + 1)
            dve.scalar_tensor_tensor(self.ft[:], self.ps_h[:, 0, 0:D], self.f[:, 2:3], self.b_res[:],
                                     ALU.mult, ALU.add).then_inc(self.s_ft, 1)
        elif stage == 4:
            dve.wait_ge(self.s_nr, t + 1)
            ch.step(dve.tensor_scalar(self.e2[:, 1:2], self.e2[:, 0:1], 1.0, None, ALU.add))
            ch.link(dve.tensor_scalar(self.e3[:], self.e2[:, 0:1], -1.0, 1.0, ALU.mult, ALU.add))
            ch.link(dve.reciprocal(self.e2[:, 1:2], self.e2[:, 1:2]))
            ch.link(dve.tensor_tensor(self.e3[:], self.e3[:], self.e2[:, 1:2], ALU.mult))
            ch.link(dve.scalar_tensor_tensor(self.f[:, 3:4], self.e3[:], MAX_NORM, self.rn[:],
                                             ALU.min, ALU.mult))
            dve.sem_inc(m.s_pass, 1)
            dve.scalar_tensor_tensor(m.X[:, t, :], self.ft[:], self.f[:, 3:4], m.X[:, t, :],
                                     ALU.mult, ALU.add).then_inc(self.s_out, 1)

    def pe(self, pe, t, stage):
        m = self.m
        if stage == 0:
            pe.wait_ge(self.s_ft, t)
            pe.wait_ge(self.s_a, t + 1)
            for k in range(2):
                mm = pe.transpose(self.ps_t[:, 0, k * P:(k + 1) * P], self.a[:, k * 128:(k + 1) * 128],
                                  m.ident[0:P, 0:P])
            mm.then_inc(self.s_pa, 1)
            pe.wait_ge(self.s_aT, t + 1)
            for j in range(2):
                for k in range(2):
                    mm = pe.matmul(self.ps_h[:, j, 0:CV // 2], self.aT[:, k, :],
                                   self.wc[:, k, j * (CV // 2):(j + 1) * (CV // 2)], start=(k == 0), stop=(k == 1))
            mm.then_inc(self.s_h, 1)
        elif stage == 1:
            pe.wait_ge(self.s_t, t + 1)
            for c in range(6):
                mm = pe.transpose(self.ps_t[:, c // 3, (c % 3) * P:(c % 3 + 1) * P],
                                  self.cat[:, c * 128:(c + 1) * 128], m.ident[0:P, 0:P])
            mm.then_inc(self.s_pt, 1)
        elif stage == 2:
            pe.wait_ge(self.s_tT, t + 1)
            for c in range(6):
                mm = pe.matmul(self.ps_h[:, c // 3, (c % 3) * 128:(c % 3 + 1) * 128], self.tT[:, c, :],
                               self.bd[:, c, :], start=True, stop=True)
            mm.then_inc(self.s_s, 1)
        elif stage == 3:
            pe.wait_ge(self.s_o, t + 1)
            for c in range(4):
                mm = pe.transpose(self.ps_t[:, 0, c * P:(c + 1) * P],
                                  self.o.rearrange("p g d -> p (g d)")[:, c * 128:(c + 1) * 128], m.ident[0:P, 0:P])
            mm.then_inc(self.s_po, 1)
        elif stage == 4:
            pe.wait_ge(self.s_oT, t + 1)
            for c in range(4):
                mm = pe.matmul(self.ps_h[:, 0, 0:D], self.oT[:, c, :], self.res[:, c, :], start=(c == 0),
                               stop=(c == 3))
            mm.then_inc(self.s_r, 1)

    ACT_STEPS = 15

    def act(self, act, ch, t, stage):
        def norm(j, src, n):
            ch.link(act.activation(self.junk[:, 0:n], src, ACT.Square, accum_out=self.n2[:, j:j + 1]))
            ch.link(act.activation(self.ln[:, j:j + 1], self.n2[:, j:j + 1], ACT.Ln, bias=self.tiny[:]))

        def factor(j):
            ch.link(act.activation(self.nn[:, j:j + 1], self.ln[:, j:j + 1], ACT.Relu, scale=0.5, bias=self.lnmax[:]))
            act.activation(self.f[:, j:j + 1], self.nn[:, j:j + 1], ACT.Exp, scale=-1.0).then_inc(self.s_f, 1)

        if stage == 0:
            act.wait_ge(self.s_pa, t + 1)
            act.activation(self.aT.rearrange("p k n -> p (k n)"), self.ps_t[:, 0, 0:2 * P], ACT.Copy
                           ).then_inc(self.s_aT, 1)
        elif stage == 1:
            act.wait_ge(self.s_hb, t + 1)
            ch.link(act.activation(self.hb[:], self.hb[:], ACT.Relu))
            norm(0, self.hb[:], CV)
            factor(0)
            act.wait_ge(self.s_f, 3 * t + 1)
            act.activation(self.cat[:, 0:CV], self.hb[:], ACT.Copy, scale=self.f[:, 0:1]).then_inc(self.s_t, 1)
        elif stage == 2:
            act.wait_ge(self.s_pt, t + 1)
            act.activation(self.tT.rearrange("p (j c) n -> p j (c n)", j=2), self.ps_t[:, :, 0:3 * P], ACT.Copy
                           ).then_inc(self.s_tT, 1)
        elif stage == 5:
            act.wait_ge(self.s_s, t + 1)
            act.wait_ge(self.s_t, t + 1)
            ch.link(act.activation(self.cat[:, CV:].rearrange("p (j n) -> p j n", j=2), self.ps_h[:, :, 0:CV // 2],
                                   ACT.Copy))
            norm(1, self.cat[:], 2 * CV)
            factor(1)
        elif stage == 3:
            act.wait_ge(self.s_po, t + 1)
            act.activation(self.oT.rearrange("p c n -> p (c n)"), self.ps_t[:, 0, 0:4 * P], ACT.Copy
                           ).then_inc(self.s_oT, 1)
            act.wait_ge(self.s_o, t + 1)
            norm(2, self.o.rearrange("p g d -> p (g d)"), 2 * D)
            factor(2)
        elif stage == 4:
            act.wait_ge(self.s_ft, t + 1)
            norm(3, self.ft[:], D)
            ch.link(act.activation(self.nn[:, 3:4], self.ln[:, 3:4], ACT.Exp, scale=0.5))
            ch.link(act.activation(self.rn[:], self.ln[:, 3:4], ACT.Exp, scale=-0.5))
            act.activation(self.e2[:, 0:1], self.nn[:, 3:4], ACT.Exp, scale=-2.0).then_inc(self.s_nr, 1)




GB = 4


class Blk:

    def __init__(self, i, x):
        self.k, self.half, self.quart = GB * i + x, GB // 2 * i + x // 2, i + x // GB
        self.b, self.g = x % 2, x % GB


@phase
def edge_layer(nc, m, tag, heads, width, table, rows, pieces, att=None, mixer=None, tile0=0):
    hb = CB * heads
    tw = table.shape[1]
    rw = rows.shape[1]
    pw = width + 2 * heads
    vw = width + heads
    per_bank = 4 if 4 * vw <= 512 else 1
    fills = CB // per_bank
    cw = width // heads
    blocks = NC // CB
    trips = blocks // 2
    S = {n: m.sem(f"{tag}_{n}") for n in ("ld", "m", "xr", "lg", "dc", "pt", "mx", "pm", "d", "ex", "v", "agg", "r")}
    s_db = [m.sem(f"{tag}_db{b}") for b in range(2)]
    s_gt = [m.gather_sem(f"{tag}_gt{g}") for g in range(GB)]
    s_st = [m.sem(f"{tag}_st{b}") for b in range(2)]
    c_dve, c_act, c_pool = m.sem(f"{tag}_dve"), m.sem(f"{tag}_act"), m.sem(f"{tag}_pool")
    with ExitStack() as st:
        def sb(name, shape, dt=F32):
            return st.enter_context(nc.sbuf_tensor(f"{tag}_{name}", shape, dt))
        idx = [sb(f"idx{g}", [P, CB], I32) for g in range(GB)]
        gt = [sb(f"gt{g}", [P, CB, tw]) for g in range(GB)]
        if mixer:
            mixer.banks(st, tag)
        dstb = [sb(f"dstb{b}", [P, CB, P], I32) for b in range(2)]
        er = [sb(f"er{b}", [P, CB, rw]) for b in range(2)]
        same = [sb(f"same{g}", [P, CB, P]) for g in range(GB)]
        dcol = [sb(f"dcol{b}", [P, CB, heads]) for b in range(2)]
        z = sb("z", [P, CB * rw])
        lg = [sb(f"lg{b}", [P, hb]) for b in range(2)]
        dr = sb("dr", [hb, P])
        gate = sb("gate", [hb, P + 1])
        fwd, bwd = sb("fwd", [hb, P]), sb("bwd", [hb, P])
        mx = [sb(f"mx{b}", [hb, P]) for b in range(2)]
        dd = [sb(f"dd{b}", [P, CB, heads]) for b in range(2)]
        vals = [sb(f"vals{b}", [P, CB, vw]) for b in range(2)]
        out = [sb(f"out{b}", [P, CB, pw]) for b in range(2)]
        ps_a = st.enter_context(nc.psum_tensor(f"{tag}_pa", [P, 512], F32))
        ps_t = st.enter_context(nc.psum_tensor(f"{tag}_pt", [128, 512], F32))
        ps_o = [st.enter_context(nc.psum_tensor(f"{tag}_po{j}", [P, 512], F32)) for j in range(2)]
        MO = 2 * 128
        dst_v = m.dst.rearrange("(k n) -> k n", n=CB * P)
        rows_v = rows.rearrange("(k c p) w -> k p c w", c=CB, p=P)
        pieces_v = pieces.rearrange("(k c p) w -> k p c w", c=CB, p=P)
        block = st.enter_context(nc.Block())

        @block.sync
        def _(sp):
            sp.wait_ge(m.s_zero, 464)
            with sp.Fori(0, trips) as i:
                for b in range(2):
                    k = 2 * i + b
                    sp.wait_ge(S["m"], free(k))
                    sp.dma_start(dstb[b].rearrange("p c e -> p (c e)"),
                                 dst_v[k].unsqueeze(0).to_broadcast([P, CB * P])).then_inc(s_db[b], 16)
                    sp.wait_ge(S["xr"], free(k))
                    sp.dma_start(er[b][:], rows_v[k]).then_inc(s_db[b], 16)

        @block.gpsimd
        def _(pool):
            ch = Chain(pool, c_pool)
            with pool.Fori(0, blocks // GB) as i:
                ch.loop(i, GB)
                for g in range(GB):
                    k = GB * i + g
                    pool.wait_ge(s_gt[g], 16 * CB * i)
                    pool.sem_inc(m.s_pass, 1)
                    ch.link(pool.tensor_copy(idx[g][:], m.srcT[:, bass.ds(k * CB, CB)]))
                    pool.wait_ge(S["v"], k + 1)
                    pool.sem_inc(m.s_pass, 1)
                    for c in range(CB):
                        pool.indirect_dma_start(out=gt[g][:, c, :], out_offset=None, in_=table,
                                                in_offset=bass.IndirectOffsetOnAxis(ap=idx[g][:, c:c + 1], axis=0)
                                                ).then_inc(s_gt[g], 16)
            ch.end(blocks // GB)

        def steps(eng, step, ch=None, per=0):
            trips = (blocks - 1) // GB

            def trip(i, early, late):
                for pos in range(GB):
                    step(*(Blk(i, x) if not isinstance(i, int) or GB * i + x < blocks else None
                           for x in (pos, pos + 1, pos + 2, pos + 3)), pos, early, late)
            step(None, Blk(0, 0), Blk(0, 1), Blk(0, 2), None, None, None)
            trip(0, tile0, None)
            with eng.Fori(1, trips) as i:
                if ch is not None:
                    ch.loop(i - 1, per)
                trip(i, tile0 + i, tile0 + i - 1)
            if ch is not None:
                ch.end(trips - 1)
            trip(trips, tile0 + trips, tile0 + trips - 1)
            for pos in range(2):
                step(None, None, None, None, pos, None, tile0 + trips)

        @block.vector
        def _(dve):
            ch = Chain(dve, c_dve)
            dve.sem_inc(S["m"], DEPTH)
            dve.sem_inc(S["v"], GB)
            dve.sem_inc(S["mx"], DEPTH)
            dve.sem_inc(S["lg"], DEPTH)
            dve.sem_inc(S["d"], 2 * DEPTH)
            ch.link(dve.memset(gate[:], -BIG))

            def same_dst(x):
                dve.wait_ge(s_db[x.b], 32 * x.half + 32)
                dve.wait_ge(S["agg"], fills * free(x.k))
                dve.tensor_tensor(same[x.g][:], dstb[x.b][:],
                                  m.dstT[:, bass.ds(x.k * CB, CB)].unsqueeze(2).to_broadcast([P, CB, P]),
                                  ALU.is_equal).then_inc(S["m"], 1)
                dve.wait_ge(S["pt"], free(x.k))
                dve.sem_inc(m.s_pass, 1)
                dve.tensor_copy(dcol[x.b][:], m.dstT[:, bass.ds(x.k * CB, CB)].unsqueeze(2)
                                .to_broadcast([P, CB, heads])).then_inc(S["dc"], 1)

            def logits(x):
                dve.wait_ge(S["xr"], ready(x.k))
                dve.wait_ge(s_gt[x.g], 16 * CB * (x.quart + 1))
                rows_ = gt[x.g]
                if att is not None:
                    ch.link(dve.tensor_tensor(z[:], ps_a[:, 0:CB * rw], rows_.rearrange("p c w -> p (c w)"), ALU.add))
                    ch.link(dve.scalar_tensor_tensor(z[:], z[:], 0.2, z[:], ALU.mult, ALU.max))
                    ch.link(dve.tensor_tensor(z[:], z[:], att[:], ALU.mult))
                    dve.tensor_reduce(lg[x.b].rearrange("p (c h) -> p c h", c=CB),
                                      z.rearrange("p (c h k) -> p c h k", c=CB, h=heads), AX.X, ALU.add
                                      ).then_inc(S["lg"], 1)
                else:
                    ch.link(dve.tensor_tensor(z.rearrange("p (c h) -> p c h", c=CB),
                                              ps_a[:, 0:CB * rw].rearrange("p (c h) -> p c h", c=CB),
                                              rows_[:, :, width:width + heads], ALU.add))
                    dve.scalar_tensor_tensor(lg[x.b][:], z[:], 0.2, z[:], ALU.mult, ALU.max).then_inc(S["lg"], 1)

            def maxima(x):
                dve.wait_ge(S["pt"], ready(x.k))
                ch.link(dve.tensor_copy(dr[:], ps_t[0:hb, 128:128 + P]))
                ch.link(dve.tensor_tensor(gate[:, 1:P], dr[:, 1:P], dr[:, 0:P - 1], ALU.is_equal))
                ch.link(dve.tensor_scalar(gate[:, 1:P], gate[:, 1:P], 2 * BIG, -BIG, ALU.mult, ALU.add))
                ch.step(dve.tensor_tensor_scan(fwd[:], gate[:, 0:P], ps_t[0:hb, 0:P], -BIG, ALU.min, ALU.max))
                ch.link(dve.tensor_tensor_scan(bwd[:, ::-1], gate[:, P:0:-1], ps_t[0:hb, 0:P][:, ::-1], -BIG,
                                               ALU.min, ALU.max))
                dve.wait_ge(S["pm"], free(x.k))
                dve.tensor_tensor(mx[x.b][:], fwd[:], bwd[:], ALU.max).then_inc(S["mx"], 1)

            def shift(x):
                b = x.b
                dve.wait_ge(S["pm"], ready(x.k))
                dve.wait_ge(S["ex"], free(x.k))
                dve.tensor_tensor(dd[b].rearrange("p c h -> p (c h)"), lg[b][:], ps_t[0:P, MO:MO + hb],
                                  ALU.subtract).then_inc(S["d"], 1)
                dve.wait_ge(s_st[b], 16 * x.half)
                dve.tensor_copy(out[b][:, :, vw:pw], ps_t[0:P, MO:MO + hb].rearrange("p (c h) -> p c h", c=CB)
                                ).then_inc(S["d"], 1)

            def weigh(x):
                dve.wait_ge(S["ex"], ready(x.k))
                dve.tensor_tensor(vals[x.b][:, :, 0:width].rearrange("p c (h k) -> p c h k", h=heads),
                                  gt[x.g][:, :, 0:width].rearrange("p c (h k) -> p c h k", h=heads),
                                  vals[x.b][:, :, width:vw].unsqueeze(3).to_broadcast([P, CB, heads, cw]),
                                  ALU.mult).then_inc(S["v"], 1)

            def step(prev, cur, nxt, coming, pos, early, late):
                def mix(at, stage, tile=early):
                    if mixer and pos == at and tile is not None:
                        mixer.dve(dve, ch, tile, stage)
                mix(0, 0)
                if cur:
                    logits(cur)
                mix(1, 1)
                if prev:
                    weigh(prev)
                if cur:
                    maxima(cur)
                mix(0, 3, late)
                mix(1, 4, late)
                if coming:
                    same_dst(coming)
                if cur:
                    shift(cur)
                mix(3, 2)
            same_dst(Blk(0, 0))
            same_dst(Blk(0, 1))
            steps(dve, step, ch, GB * ((3 if att is not None else 1) + 5) + (Mixer.DVE_STEPS if mixer else 0))

        @block.tensor
        def _(pe):
            pe.sem_inc(S["xr"], DEPTH)
            pe.sem_inc(S["pt"], DEPTH)
            pe.sem_inc(S["pm"], DEPTH)
            pe.sem_inc(S["agg"], fills * GB)

            def spread(x):
                pe.wait_ge(S["m"], ready(x.k))
                pe.wait_ge(S["lg"], ready(x.k) - 1)
                pe.wait_ge(s_db[x.b], 32 * x.half + 32)
                for c in range(CB):
                    mm = pe.matmul(ps_a[:, c * rw:(c + 1) * rw], same[x.g][:, c, :], er[x.b][:, c, :],
                                   start=True, stop=True)
                mm.then_inc(S["xr"], 1)

            def rows_of(x):
                pe.wait_ge(S["lg"], ready(x.k))
                pe.wait_ge(S["dc"], x.k + 1)
                pe.wait_ge(S["d"], 2 * ready(x.k) - 2)
                pe.sem_inc(m.s_pass, 1)
                pe.transpose(ps_t[0:hb, 0:P], lg[x.b][:], m.ident[0:P, 0:P])
                pe.transpose(ps_t[0:hb, 128:128 + P], dcol[x.b].rearrange("p c h -> p (c h)"), m.ident[0:P, 0:P]
                             ).then_inc(S["pt"], 1)

            def columns(x):
                pe.wait_ge(S["mx"], ready(x.k))
                pe.sem_inc(m.s_pass, 1)
                pe.transpose(ps_t[0:P, MO:MO + hb], mx[x.b][:], m.ident[0:hb, 0:hb]).then_inc(S["pm"], 1)

            def aggregate(x, half):
                if half == 0:
                    pe.wait_ge(S["v"], x.k + GB + 1)
                for f in range(half * fills // 2, (half + 1) * fills // 2):
                    pe.wait_ge(S["r"], fills * x.k + f + 1)
                    for c in range(per_bank):
                        cc = f * per_bank + c
                        mm = pe.matmul(ps_o[f % 2][:, c * vw:(c + 1) * vw], same[x.g][:, cc, :], vals[x.b][:, cc, :],
                                       start=True, stop=True)
                    mm.then_inc(S["agg"], 1)

            def step(prev, cur, nxt, coming, pos, early, late):
                def mix(at, stage, tile=early):
                    if mixer and pos == at and tile is not None:
                        mixer.pe(pe, tile, stage)
                mix(0, 3, late)
                if cur:
                    rows_of(cur)
                mix(0, 4, late)
                mix(3, 2)
                if nxt:
                    spread(nxt)
                if cur:
                    columns(cur)
                if prev:
                    aggregate(prev, 0)
                mix(2, 1)
                mix(0, 0)
                if prev:
                    aggregate(prev, 1)
            spread(Blk(0, 0))
            steps(pe, step)

        @block.scalar
        def _(act):
            ch = Chain(act, c_act)
            act.sem_inc(S["ex"], DEPTH)
            act.sem_inc(S["r"], DEPTH)
            act.preload_act_table_set(NLE)

            def expo(x):
                act.wait_ge(S["d"], 2 * ready(x.k) - 1)
                act.wait_ge(S["agg"], fills * (x.k + GB - 1))
                act.activation(vals[x.b][:, :, width:vw], dd[x.b][:], ACT.Exp).then_inc(S["ex"], 1)

            def evacuate(x, half):
                if half == 0:
                    act.wait_ge(s_st[x.b], 16 * x.half)
                for f in range(half * fills // 2, (half + 1) * fills // 2):
                    act.wait_ge(S["agg"], fills * (x.k + GB) + f + 1)
                    act.activation(out[x.b][:, f * per_bank:(f + 1) * per_bank, 0:vw],
                                   ps_o[f % 2][:, 0:per_bank * vw].rearrange("p (c w) -> p c w", c=per_bank),
                                   ACT.Copy).then_inc(S["r"], 1)
                if half == 1:
                    act.wait_ge(S["r"], fills * (x.k + 1) + DEPTH)
                    act.wait_ge(S["d"], 2 * ready(x.k))
                    act.dma_start(pieces_v[x.k], out[x.b][:]).then_inc(s_st[x.b], 16)

            def step(prev, cur, nxt, coming, pos, early, late):
                def mix(at, stage, tile=early):
                    if mixer and pos == at and tile is not None:
                        mixer.act(act, ch, tile, stage)
                mix(0, 3, late)
                mix(3, 5)
                if prev:
                    evacuate(prev, 0)
                mix(0, 0)
                mix(0, 4, late)
                if cur:
                    expo(cur)
                mix(1, 1)
                mix(2, 2)
                if prev:
                    evacuate(prev, 1)
            steps(act, step, ch, Mixer.ACT_STEPS if mixer else 0)
            for b in range(2):
                act.wait_ge(s_st[b], 16 * trips)




@phase
def join_chunks(nc, m, tag, heads, width, pieces, rest):
    vw, pw = width + heads, width + 2 * heads
    s_ld, s_t, s_mr, s_mx, s_b, s_dd, s_ex, s_fp, s_m2, s_mm, s_ev, s_o = (
        m.sem(f"{tag}_{n}") for n in ("ld", "t", "mr", "mx", "b", "dd", "ex", "fp", "m2", "mm", "ev", "o"))
    c_dve = m.sem(f"{tag}_dve")
    with ExitStack() as st:
        def sb(name, shape, dt=F32):
            return st.enter_context(nc.sbuf_tensor(f"{tag}_{name}", shape, dt))
        fp = sb("fp", [CP, CK, pw])
        mrow, fwd, bwd, full = (sb(n, [heads, NC]) for n in ("mrow", "fwd", "bwd", "full"))
        gate = sb("gate", [heads, NC + 1])
        fm = sb("fm", [CP, CK, heads])
        dd = sb("dd", [CP, CK, heads])
        m2 = sb("m2", [CP, CK, NC])
        bt = sb("bt", [CP, CK, pw])
        ps_r = st.enter_context(nc.psum_tensor(f"{tag}_pr", [128, 2, 512], F32))
        ps_c = st.enter_context(nc.psum_tensor(f"{tag}_pc", [128, 512], F32))
        ps_m = [st.enter_context(nc.psum_tensor(f"{tag}_pm{j}", [128, 512], F32)) for j in range(2)]
        HC = NC // 2
        block = st.enter_context(nc.Block())

        @block.sync
        def _(sp):
            sp.dma_start(fp[:], pieces.rearrange("(k p e) w -> p k e w", k=CK, p=CP)[:, :, 0, :]).then_inc(s_ld, 16)
            sp.wait_ge(s_ev, 1 + CK)
            sp.dma_start(rest.rearrange("(k p) w -> p k w", p=CP), bt[:]).then_inc(s_o, 16)
            sp.wait_ge(s_o, 16)

        @block.tensor
        def _(pe):
            pe.wait_ge(s_ld, 16)
            for k in range(CK):
                mm = pe.transpose(ps_r[0:heads, k // 4, (k % 4) * CP:(k % 4 + 1) * CP], fp[:, k, vw:pw],
                                  m.ident[0:CP, 0:CP])
            mm.then_inc(s_t, 1)
            pe.wait_ge(s_mx, 1)
            for k in range(CK):
                mm = pe.transpose(ps_c[0:CP, k * heads:(k + 1) * heads], full[:, k * CP:(k + 1) * CP],
                                  m.ident[0:heads, 0:heads])
            mm.then_inc(s_b, 1)
            pe.wait_ge(s_fp, 2)
            pe.wait_ge(s_m2, CK)
            for k in range(CK):
                if k >= 2:
                    pe.wait_ge(s_ev, k - 1)
                for kk in range(CK):
                    mm = pe.matmul(ps_m[k % 2][0:CP, 0:vw], m2[:, kk, k * CP:(k + 1) * CP], fp[:, kk, 0:vw],
                                   start=(kk == 0), stop=(kk == CK - 1))
                mm.then_inc(s_mm, 1)

        @block.scalar
        def _(act):
            act.wait_ge(s_dd, 1)
            act.activation(dd[:], dd[:], ACT.Exp).then_inc(s_ex, 1)

        @block.vector
        def _(dve):
            ch = Chain(dve, c_dve)
            ch.link(dve.memset(gate[:], -BIG))
            ch.link(dve.tensor_tensor(gate[:, 1:NC], m.seg_row[0:heads, 1:NC], m.seg_row[0:heads, 0:NC - 1],
                                      ALU.is_equal))
            ch.link(dve.tensor_scalar(gate[:, 1:NC], gate[:, 1:NC], 2 * BIG, -BIG, ALU.mult, ALU.add))
            for k in range(CK):
                dve.tensor_scalar(m2[:, k, :], m.seg_row[:], m.seg_col[:, k:k + 1], None, ALU.is_equal
                                  ).then_inc(s_m2, 1)
            dve.wait_ge(s_t, 1)
            ch.link(dve.tensor_copy(mrow.rearrange("h (j n) -> h j n", j=2), ps_r[0:heads, :, 0:HC]))
            ch.step(dve.tensor_tensor_scan(fwd[:], gate[:, 0:NC], mrow[:], -BIG, ALU.min, ALU.max))
            ch.link(dve.tensor_tensor_scan(bwd[:, ::-1], gate[:, NC:0:-1], mrow[:, ::-1], -BIG, ALU.min, ALU.max))
            dve.tensor_tensor(full[:], fwd[:], bwd[:], ALU.max).then_inc(s_mx, 1)
            dve.wait_ge(s_b, 1)
            ch.link(dve.tensor_copy(fm.rearrange("p k h -> p (k h)"), ps_c[0:CP, 0:CK * heads]))
            dve.tensor_tensor(dd[:], fp[:, :, vw:pw], fm[:], ALU.subtract).then_inc(s_dd, 1)
            dve.wait_ge(s_ex, 1)
            for k in range(CK):
                ins = dve.tensor_tensor(fp[:, k, 0:width].rearrange("p (h c) -> p h c", h=heads),
                                        fp[:, k, 0:width].rearrange("p (h c) -> p h c", h=heads),
                                        dd[:, k, :].unsqueeze(2).to_broadcast([CP, heads, width // heads]), ALU.mult)
            ins.then_inc(s_fp, 1)
            dve.tensor_tensor(fp[:, :, width:vw], fp[:, :, width:vw], dd[:], ALU.mult).then_inc(s_fp, 1)
            for k in range(CK):
                dve.wait_ge(s_mm, k + 1)
                dve.tensor_copy(bt[:, k, 0:vw], ps_m[k % 2][0:CP, 0:vw]).then_inc(s_ev, 1)
            dve.tensor_copy(bt[:, :, vw:pw], fm[:]).then_inc(s_ev, 1)



TG = 5


@phase
def node_groups(nc, m, tag, heads, width, pieces, rest, bias, w=None, cols=0, bias2=None, last=False,
                gathered=None, spread=None, slots=None, self_loops=None):
    vw, pw = width + heads, width + 2 * heads
    cw = width // heads
    np_ = 3 if self_loops else 2
    trips = NT // TG // 2
    names = ("pc", "dd", "ex", "h", "ht", "hs", "mm", "tab", "ix", "fin")
    S = {n: m.sem(f"{tag}_{n}") for n in names}
    s_g = [m.gather_sem(f"{tag}_g{b}") for b in range(2)]
    s_l = [m.sem(f"{tag}_l{b}") for b in range(2)]
    s_o = [m.sem(f"{tag}_o{b}") for b in range(2)]
    s_sc = [m.gather_sem(f"{tag}_sc{b}") for b in range(2)]
    c_dve, c_act, c_pool = m.sem(f"{tag}_dve"), m.sem(f"{tag}_act"), m.sem(f"{tag}_pool")
    with ExitStack() as st:
        def sb(name, shape, dt=F32):
            return st.enter_context(nc.sbuf_tensor(f"{tag}_{name}", shape, dt))
        idx = [sb(f"idx{b}", [P, 3, TG], I32) for b in range(2)]
        first = [sb(f"first{b}", [P, TG, pw]) for b in range(2)]
        more = [sb(f"more{b}", [P, TG, pw]) for b in range(2)]
        mm_ = sb("mm", [P, TG, heads])
        dd = [sb(f"dd{b}", [P, np_, TG, heads]) for b in range(2)]
        den = sb("den", [P, TG, heads])
        h = [sb(f"h{b}", [P, TG, width]) for b in range(2)]
        if self_loops:
            own_h = [sb(f"oh{b}", [P, TG, vw]) for b in range(2)]
            own_d = [sb(f"od{b}", [P, TG, heads]) for b in range(2)]
            neg = sb("neg", [P, TG, width])
        if w is not None:
            per = 512 // cols
            nb = -(-TG // per)
            hT = [sb(f"hT{b}", [width, TG, P]) for b in range(2)]
            tab = [sb(f"tab{b}", [P, TG, cols if last else cols // 2]) for b in range(2)]
            own = [sb(f"own{b}", [P, TG, cols // 2]) for b in range(2)] if not last else None
            ps_t = st.enter_context(nc.psum_tensor(f"{tag}_pt", [128, 2, 512], F32))
            ps_w = st.enter_context(nc.psum_tensor(f"{tag}_pw", [P, nb, 512], F32))
        block = st.enter_context(nc.Block())

        def spread_heads(ap, c):
            return ap.unsqueeze(3).to_broadcast([P, TG, heads, c])

        def by_head(ap):
            return ap.rearrange("p t (h c) -> p t h c", h=heads)

        @block.gpsimd
        def _(pool):
            ch = Chain(pool, c_pool)
            limit = pool.to_reg(E - 1)

            def gather(i):
                for b in range(2):
                    q = 2 * i + b
                    pool.wait_ge(s_g[b], 32 * TG * i)
                    pool.sem_inc(m.s_pass, 1)
                    for j, src in enumerate((m.start_i, m.next_i)):
                        ch.step(pool.tensor_copy(idx[b][:, j, :], src[:, bass.ds(q * TG, TG)]))
                    ch.settle()
                    pool.wait_ge(S["pc"], free(q))
                    pool.sem_inc(m.s_pass, 1)
                    for j in range(TG):
                        pool.indirect_dma_start(out=first[b][:, j, :], out_offset=None, in_=pieces,
                                                in_offset=bass.IndirectOffsetOnAxis(ap=idx[b][:, 0, j:j + 1], axis=0)
                                                ).then_inc(s_g[b], 16)
                        pool.indirect_dma_start(out=more[b][:, j, :], out_offset=None, in_=rest,
                                                in_offset=bass.IndirectOffsetOnAxis(ap=idx[b][:, 1, j:j + 1], axis=0)
                                                ).then_inc(s_g[b], 16)

            def scatter(i):
                for b in range(2):
                    q = 2 * i + b
                    pool.wait_ge(s_sc[b], 16 * TG * i)
                    pool.sem_inc(m.s_pass, 1)
                    ch.link(pool.tensor_copy(idx[b][:, 2, :], m.slot_i[:, bass.ds(q * TG, TG)]))
                    pool.wait_ge(S["tab"], 2 * ready(q))
                    pool.sem_inc(m.s_pass, 1)
                    for j in range(TG):
                        pool.indirect_dma_start(out=slots, in_=own[b][:, j, :], in_offset=None,
                                                out_offset=bass.IndirectOffsetOnAxis(ap=idx[b][:, 2, j:j + 1],
                                                                                     axis=0),
                                                bounds_check=limit, oob_is_err=False).then_inc(s_sc[b], 16)
            gather(0)
            with pool.Fori(1, trips) as i:
                ch.loop(i - 1, 4 if slots is None else 6)
                gather(i)
                if slots is not None:
                    scatter(i - 1)
            ch.end(trips - 1)
            if slots is not None:
                scatter(trips - 1)
                for b in range(2):
                    pool.wait_ge(s_sc[b], 16 * TG * trips)

        @block.sync
        def _(sp):
            with sp.Fori(0, trips) as i:
                for b in range(2):
                    q = 2 * i + b
                    if self_loops:
                        hv, dv = (x.rearrange("(g t p) w -> g p t w", t=TG, p=P) for x in self_loops)
                        sp.wait_ge(S["pc"], free(q))
                        sp.dma_start(own_h[b][:], hv[q]).then_inc(s_l[b], 16)
                        sp.dma_start(own_d[b][:], dv[q]).then_inc(s_l[b], 16)
                    if slots is not None:
                        sp.wait_ge(S["tab"], 2 * ready(q))
                        for x, v in ((tab[b], gathered), (own[b], spread)):
                            sp.dma_start(v.rearrange("(g t p) w -> g p t w", t=TG, p=P)[q], x[:]).then_inc(s_o[b], 16)
            if slots is not None:
                for b in range(2):
                    sp.wait_ge(s_o[b], 32 * trips)

        @block.vector
        def _(dve):
            ch = Chain(dve, c_dve)
            for n, c in (("pc", 1), ("dd", 1), ("h", 1), ("tab", 2)):
                dve.sem_inc(S[n], c * DEPTH)

            def weights(q, b):
                a1, a2 = first[b], more[b]
                ts = bass.ds(q * TG, TG)
                dve.wait_ge(s_g[b], 32 * TG * (i_ + 1))
                dve.wait_ge(S["ex"], free(q))
                ch.link(dve.tensor_tensor(dd[b][:, 1], a2[:, :, vw:pw],
                                          m.gate2[:, ts].unsqueeze(2).to_broadcast([P, TG, heads]), ALU.min))
                if self_loops:
                    dve.wait_ge(s_l[b], 32 * (i_ + 1))
                    ch.link(dve.tensor_tensor(dd[b][:, 0], a1[:, :, vw:pw],
                                              m.gate1[:, ts].unsqueeze(2).to_broadcast([P, TG, heads]), ALU.min))
                    ch.step(dve.tensor_tensor(mm_[:], dd[b][:, 0], dd[b][:, 1], ALU.max))
                    ch.link(dve.tensor_tensor(dd[b][:, 2], own_h[b][:, :, width:vw], own_d[b][:], ALU.add))
                    ch.link(dve.scalar_tensor_tensor(dd[b][:, 2], dd[b][:, 2], 0.2, dd[b][:, 2], ALU.mult, ALU.max))
                    ch.link(dve.tensor_tensor(mm_[:], mm_[:], dd[b][:, 2], ALU.max))
                    ch.link(dve.tensor_tensor(dd[b][:, 0], dd[b][:, 0], mm_[:], ALU.subtract))
                    ch.link(dve.tensor_tensor(dd[b][:, 2], dd[b][:, 2], mm_[:], ALU.subtract))
                else:
                    ch.link(dve.tensor_tensor(mm_[:], a1[:, :, vw:pw], dd[b][:, 1], ALU.max))
                    ch.step(dve.tensor_tensor(dd[b][:, 0], a1[:, :, vw:pw], mm_[:], ALU.subtract))
                dve.tensor_tensor(dd[b][:, 1], dd[b][:, 1], mm_[:], ALU.subtract).then_inc(S["dd"], 1)
            WEIGHTS = 8 if self_loops else 3

            def sums(q, b):
                ts = bass.ds(q * TG, TG)
                a = [first[b], more[b]] + ([own_h[b]] if self_loops else [])
                hb_, hs = m.has[:, ts], h[b]
                dve.wait_ge(S["ex"], ready(q))
                ch.link(dve.tensor_tensor(dd[b][:, 0], dd[b][:, 0], hb_.unsqueeze(2).to_broadcast([P, TG, heads]),
                                          ALU.mult))
                for j, x in enumerate(a):
                    ch.step(dve.tensor_tensor(by_head(x[:, :, 0:width]), by_head(x[:, :, 0:width]),
                                              spread_heads(dd[b][:, j], cw), ALU.mult))
                    if j < 2:
                        ch.step(dve.tensor_tensor(x[:, :, width:vw], x[:, :, width:vw], dd[b][:, j], ALU.mult))
                ch.settle()
                ch.step(dve.tensor_tensor(a[0][:, :, 0:vw], a[0][:, :, 0:vw], a[1][:, :, 0:vw], ALU.add))
                if self_loops:
                    ch.settle()
                    ch.step(dve.tensor_tensor(a[0][:, :, 0:width], a[0][:, :, 0:width], a[2][:, :, 0:width], ALU.add))
                    ch.link(dve.tensor_tensor(den[:], a[0][:, :, width:vw], dd[b][:, 2], ALU.add))
                    ch.link(dve.tensor_scalar(den[:], den[:], 1e-16, None, ALU.add))
                else:
                    ch.settle()
                    ch.link(dve.tensor_tensor(den[:], a[0][:, :, width:vw],
                                              hb_.unsqueeze(2).to_broadcast([P, TG, heads]), ALU.subtract))
                    ch.link(dve.tensor_scalar(den[:], den[:], 1.0, None, ALU.add))
                ch.link(dve.reciprocal(den[:], den[:]))
                dve.wait_ge(S["ht" if not self_loops else "fin"], free(q) if not self_loops else q)
                ch.link(dve.tensor_tensor(by_head(hs[:]), by_head(a[0][:, :, 0:width]), spread_heads(den[:], cw),
                                          ALU.mult))
                dve.sem_inc(S["pc"], 1)
                ch.link(dve.tensor_tensor(hs[:], hs[:], bias[:, 0:width].unsqueeze(1).to_broadcast([P, TG, width]),
                                          ALU.add))
                if not self_loops:
                    dve.tensor_scalar(hs[:], hs[:], 0.0, None, ALU.max).then_inc(S["h"], 1)
                    return
                dve.tensor_scalar(neg[:], hs[:], 0.0, None, ALU.min).then_inc(S["h"], 1)
                ch.link(dve.tensor_scalar(hs[:], hs[:], 0.0, -1.0, ALU.max, ALU.add))
                dve.wait_ge(S["hs"], q + 1)
                ch.link(dve.tensor_tensor(hs[:], hs[:], neg[:], ALU.add))
                dve.tensor_tensor(m.X[:, ts, :], m.X[:, ts, :], hs[:], ALU.add).then_inc(S["fin"], 1)
            SUMS = 15 if self_loops else 11

            def tail(q, b):
                ts = bass.ds(q * TG, TG)
                dve.wait_ge(S["mm"], q + 1)
                if last:
                    for j in range(nb):
                        n = min(per, TG - j * per)
                        ins = dve.tensor_tensor(tab[b][:, j * per:j * per + n, :],
                                                ps_w[:, j, 0:n * cols].rearrange("p (t n) -> p t n", t=n),
                                                bias2[:, 0:cols].unsqueeze(1).to_broadcast([P, n, cols]), ALU.add)
                        ch.step(ins)
                    ch.settle()
                    dve.sem_inc(S["tab"], 2)
                    dve.wait_ge(S["fin"], q + 1)
                    ch.link(dve.tensor_tensor(m.X[:, ts, :], m.X[:, ts, :], tab[b][:], ALU.add))
                    return
                dve.wait_ge(s_o[b], 32 * i_)
                dve.wait_ge(s_sc[b], 16 * TG * i_)
                half = cols // 2
                for x, lo in ((tab[b], 0), (own[b], half)):
                    for j in range(nb):
                        n = min(per, TG - j * per)
                        ch.step(dve.tensor_tensor(x[:, j * per:j * per + n, :],
                                                  ps_w[:, j, 0:n * cols].rearrange("p (t n) -> p t n", t=n)
                                                  [:, :, lo:lo + half],
                                                  bias2[:, lo:lo + half].unsqueeze(1).to_broadcast([P, n, half]),
                                                  ALU.add))
                ch.settle()
                dve.sem_inc(S["tab"], 2)
            TAIL = 0 if w is None else nb + 1 if last else 2 * nb

            with dve.Fori(0, trips) as i_:
                ch.loop(i_, 2 * (WEIGHTS + SUMS + TAIL))
                for b in range(2):
                    weights(2 * i_ + b, b)
                    sums(2 * i_ + b, b)
                if w is not None:
                    tail(2 * i_, 0)
                    tail(2 * i_ + 1, 1)
            ch.end(trips)

        @block.scalar
        def _(act):
            act.sem_inc(S["ex"], DEPTH)
            with act.Fori(0, trips) as i_:
                for b in range(2):
                    q = 2 * i_ + b
                    act.wait_ge(S["dd"], ready(q))
                    act.activation(dd[b].rearrange("p k t h -> p (k t h)"), dd[b].rearrange("p k t h -> p (k t h)"),
                                   ACT.Exp).then_inc(S["ex"], 1)
                    if self_loops:
                        act.wait_ge(S["h"], ready(q))
                        act.activation(neg[:], neg[:], ACT.Exp).then_inc(S["hs"], 1)
                        continue
                    act.wait_ge(S["ht"], ready(q))
                    act.wait_ge(S["mm"], q)
                    act.activation(hT[b][:, 0:4, :].rearrange("p t n -> p (t n)"), ps_t[0:width, 0, 0:4 * P],
                                   ACT.Copy)
                    act.activation(hT[b][:, 4, :], ps_t[0:width, 1, 0:P], ACT.Copy).then_inc(S["hs"], 1)
                if last:
                    for b in range(2):
                        q = 2 * i_ + b
                        act.wait_ge(S["tab"], 2 * ready(q))
                        act.activation(tab[b][:], tab[b][:], ACT.Sigmoid).then_inc(S["fin"], 1)

        if w is not None:
            @block.tensor
            def _(pe):
                pe.sem_inc(S["ht"], DEPTH)
                with pe.Fori(0, trips) as i_:
                    for b in range(2):
                        q = 2 * i_ + b
                        pe.wait_ge(S["h"], ready(q))
                        pe.wait_ge(S["hs"], q)
                        pe.sem_inc(m.s_pass, 1)
                        for j in range(TG):
                            mm = pe.transpose(ps_t[0:width, j // 4, (j % 4) * P:(j % 4 + 1) * P], h[b][:, j, :],
                                              m.ident[0:P, 0:P])
                        mm.then_inc(S["ht"], 1)
                        pe.wait_ge(S["hs"], q + 1)
                        pe.wait_ge(S["tab"], 2 * ready(q) - 2)
                        for j in range(TG):
                            mm = pe.matmul(ps_w[:, j // per, (j % per) * cols:(j % per + 1) * cols], hT[b][:, j, :],
                                           w[:], start=True, stop=True)
                        mm.then_inc(S["mm"], 1)




@phase
def route_weights(nc, m, tag, xT_all, wr, br, wts):
    s_xn, s_pT, s_xT = (m.sem(f"{tag}_{n}") for n in ("xn", "pT", "xT"))
    c_dve = m.sem(f"{tag}_dve")
    with ExitStack() as st:
        xn = [st.enter_context(nc.sbuf_tensor(f"{tag}_xn{b}", [P, D], F32)) for b in range(2)]
        prod = st.enter_context(nc.sbuf_tensor(f"{tag}_prod", [P, 2, D], F32))
        sums = st.enter_context(nc.sbuf_tensor(f"{tag}_sums", [P, 2], F32))
        ps_t = [st.enter_context(nc.psum_tensor(f"{tag}_pt{b}", [128, 2, P], F32)) for b in range(2)]
        block = st.enter_context(nc.Block())

        @block.vector
        def _(dve):
            ch = Chain(dve, c_dve)
            with dve.Fori(0, NT // 2) as i:
                ch.loop(i, 4)
                for b in range(2):
                    t = 2 * i + b
                    dve.wait_ge(s_pT, free(t))
                    dve.tensor_scalar(xn[b][:], m.X[:, t, :], m.mean[:, bass.ds(t, 1)], m.rstd[:, bass.ds(t, 1)],
                                      ALU.subtract, ALU.mult).then_inc(s_xn, 1)
                dve.wait_ge(s_xn, 2 * i + 2)
                for b in range(2):
                    ch.step(dve.tensor_tensor(prod[:, b, :], xn[b][:], wr[:], ALU.mult))
                ch.settle()
                ch.link(dve.tensor_reduce(sums[:], prod[:], AX.X, ALU.add))
                ch.link(dve.tensor_copy(wts[:, bass.ds(2 * i, 2)], sums[:]))
            ch.end(NT // 2)
            ch.link(dve.tensor_scalar(wts[:], wts[:], br[:, 0:1], None, ALU.add))

        @block.tensor
        def _(pe):
            pe.sem_inc(s_pT, DEPTH)
            with pe.Fori(0, NT // 2) as i:
                for b in range(2):
                    t = 2 * i + b
                    pe.wait_ge(s_xT, free(t))
                    pe.wait_ge(s_xn, t + 1)
                    pe.sem_inc(m.s_pass, 1)
                    for k in range(2):
                        mm = pe.transpose(ps_t[b][:, k, :], xn[b][:, k * 128:(k + 1) * 128], m.ident[0:P, 0:P])
                    mm.then_inc(s_pT, 1)

        @block.scalar
        def _(act):
            act.sem_inc(s_xT, DEPTH)
            with act.Fori(0, NT // 2) as i:
                for b in range(2):
                    t = 2 * i + b
                    act.wait_ge(s_pT, ready(t))
                    act.sem_inc(m.s_pass, 1)
                    act.activation(xT_all[:, :, bass.ds(t * P, P)], ps_t[b][:], ACT.Copy).then_inc(s_xT, 1)


@phase
def select_rows(nc, m, tag, wts):
    s_c, s_p, s_k = (m.sem(f"{tag}_{n}") for n in ("c", "p", "k"))
    c_dve = m.sem(f"{tag}_dve")
    BITS = 31
    with ExitStack() as st:
        def sb(name, shape, dt=F32):
            return st.enter_context(nc.sbuf_tensor(f"{tag}_{name}", shape, dt))
        u, junk, above, equal, tot, upto = (sb(n, [P, NT]) for n in ("u", "junk", "above", "equal", "tot", "upto"))
        earlier = sb("earlier", [P, P])
        cnt, need, sign, bit, left = (sb(n, [P, 1]) for n in ("cnt", "need", "sign", "bit", "left"))
        c, cand, bit_i, took = (sb(n, [P, 1], I32) for n in ("c", "cand", "bit_i", "took"))
        ps_n = st.enter_context(nc.psum_tensor(f"{tag}_pn", [P, 512], F32))
        ps_e = st.enter_context(nc.psum_tensor(f"{tag}_pe", [P, 512], F32))
        block = st.enter_context(nc.Block())

        @block.gpsimd
        def _(pool):
            pool.affine_select(out=earlier[:], in_=m.ones[0:P, 0:P], compare_op=ALU.is_gt, fill=0.0, base=0,
                               pattern=[[1, P]], channel_multiplier=-1).then_inc(s_k, 1)

        @block.tensor
        def _(pe):
            def total(n):
                pe.wait_ge(s_c, n)
                pe.sem_inc(m.s_pass, 1)
                pe.matmul(ps_n[:, 0:1], m.ones[0:P, 0:P], cnt[:], start=True, stop=True).then_inc(s_p, 1)
            total(1)
            with pe.Fori(0, BITS) as i:
                total(i + 2)
            total(BITS + 2)
            pe.wait_ge(s_k, 1)
            pe.matmul(ps_e[:, 0:NT], earlier[:], equal[:], start=True, stop=True)
            pe.matmul(ps_e[:, NT:2 * NT], m.ones[0:P, 0:P], equal[:], start=True, stop=True).then_inc(s_p, 1)

        @block.vector
        def _(dve):
            ch = Chain(dve, c_dve)

            def count(n, x, limit, op, result=junk):
                dve.tensor_scalar(result[:], x[:], limit, None, op, ALU.add, accum_out=cnt[:]).then_inc(s_c, 1)
                dve.wait_ge(s_p, n)
            ch.step(dve.memset(c[:], 0))
            ch.link(dve.memset(bit[:], float(2 ** (BITS - 1))))
            ch.link(dve.tensor_copy(bit_i[:], bit[:]))
            count(1, wts, 0.0, ALU.is_ge)
            ch.link(dve.tensor_scalar(sign[:], ps_n[:, 0:1], float(KEEP), None, ALU.is_ge))
            ch.step(dve.tensor_scalar(need[:], sign[:], 2.0 * KEEP - N - 1, float(N - KEEP + 1), ALU.mult, ALU.add))
            ch.link(dve.tensor_scalar(sign[:], sign[:], 2.0, -1.0, ALU.mult, ALU.add))
            ch.link(dve.tensor_scalar(u[:], wts[:], sign[:, 0:1], None, ALU.mult))
            with dve.Fori(0, BITS) as i:
                ch.loop(i, 5)
                ch.link(dve.tensor_tensor(cand[:], c[:], bit_i[:], ALU.bitwise_or))
                count(i + 2, u, cand[:, 0:1].bitcast(F32), ALU.is_ge)
                ch.link(dve.tensor_scalar(took[:], ps_n[:, 0:1], need[:, 0:1], bit[:, 0:1], ALU.is_ge, ALU.mult))
                ch.link(dve.tensor_tensor(c[:], c[:], took[:], ALU.bitwise_or))
                ch.link(dve.tensor_scalar(bit[:], bit[:], 0.5, None, ALU.mult))
                ch.link(dve.tensor_copy(bit_i[:], bit[:]))
            ch.end(BITS)
            ch.link(dve.tensor_tensor(sign[:], sign[:], c[:].bitcast(F32), ALU.mult))
            ch.link(dve.tensor_scalar(equal[:], wts[:], sign[:, 0:1], None, ALU.is_equal))
            count(BITS + 2, wts, sign[:, 0:1], ALU.is_gt, above)
            ch.link(dve.tensor_scalar(left[:], ps_n[:, 0:1], -1.0, float(KEEP), ALU.mult, ALU.add))
            dve.wait_ge(s_p, BITS + 3)
            ch.link(dve.tensor_copy(tot[:], ps_e[:, NT:2 * NT]))
            ch.link(dve.tensor_tensor_scan(upto[:], m.ones[0:P, 0:NT], tot[:], 0.0, ALU.mult, ALU.add))
            ch.link(dve.tensor_tensor(upto[:], upto[:], tot[:], ALU.subtract))
            ch.link(dve.tensor_tensor(upto[:], upto[:], ps_e[:, 0:NT], ALU.add))
            ch.link(dve.tensor_scalar(upto[:], upto[:], left[:, 0:1], None, ALU.is_lt))
            ch.link(dve.tensor_tensor(upto[:], upto[:], equal[:], ALU.mult))
            ch.link(dve.tensor_tensor(above[:], above[:], upto[:], ALU.add))
            ch.link(dve.tensor_tensor(wts[:], wts[:], above[:], ALU.mult))


@phase
def feed_forward(nc, m, tag, xT_all, wts, w1, b1, w2, b2):
    s_h, s_g, s_y, s_fin = (m.sem(f"{tag}_{n}") for n in ("h", "g", "y", "fin"))
    c_dve = m.sem(f"{tag}_dve")
    HB, G = HID // 128, 2 * P
    pairs = NT // 2
    trips = pairs // 2
    assert pairs == 2 * trips + 1
    with ExitStack() as st:
        def sb(name, shape, dt=F32):
            return st.enter_context(nc.sbuf_tensor(f"{tag}_{name}", shape, dt))
        hT = [sb(f"hT{b}", [128, HB, G]) for b in range(2)]
        y = sb("y", [P, 2, D])
        xn = sb("xn", [P, 2, D])
        ps_h = [st.enter_context(nc.psum_tensor(f"{tag}_ph{b}", [128, 512], F32)) for b in range(2)]
        ps_y = [st.enter_context(nc.psum_tensor(f"{tag}_py{b}", [P, 2, D], F32)) for b in range(2)]
        block = st.enter_context(nc.Block())

        @block.tensor
        def _(pe):
            def hidden(g):
                for j in range(HB):
                    if not (isinstance(g, int) and 8 * g + j < 2):
                        pe.wait_ge(s_g, HB * g + j - 1)
                        pe.sem_inc(m.s_pass, 1)
                    for k in range(2):
                        mm = pe.matmul(ps_h[j % 2][:, 0:G], w1[:, k, j * 128:(j + 1) * 128],
                                       xT_all[:, k, bass.ds(g * G, G)], start=(k == 0), stop=(k == 1))
                    mm.then_inc(s_h, 1)

            def product(g, b):
                pe.wait_ge(s_fin, free(g))
                pe.wait_ge(s_g, HB * (g + 1))
                pe.sem_inc(m.s_pass, 1)
                for u in range(2):
                    for j in range(HB):
                        mm = pe.matmul(ps_y[b][:, u, :], hT[b][:, j, u * P:(u + 1) * P], w2[:, j, :],
                                       start=(j == 0), stop=(j == HB - 1))
                mm.then_inc(s_y, 1)
            pe.sem_inc(s_y, DEPTH)
            hidden(0)
            with pe.Fori(0, trips) as i:
                hidden(2 * i + 1)
                product(2 * i, 0)
                hidden(2 * i + 2)
                product(2 * i + 1, 1)
            product(2 * trips, 0)

        @block.scalar
        def _(act):
            act.preload_act_table_set("gelu_apprx_tanh_and_others")

            def gelu(g, b):
                act.wait_ge(s_y, free(g))
                for j in range(HB):
                    act.wait_ge(s_h, HB * g + j + 1)
                    act.activation(hT[b][:, j, :], ps_h[j % 2][:, 0:G], ACT.Gelu_apprx_tanh, bias=b1[:, j:j + 1]
                                   ).then_inc(s_g, 1)
            with act.Fori(0, trips) as i:
                gelu(2 * i, 0)
                gelu(2 * i + 1, 1)
            gelu(2 * trips, 0)

        @block.vector
        def _(dve):
            ch = Chain(dve, c_dve)
            dve.sem_inc(s_fin, DEPTH)

            def finish(g, b):
                ts = bass.ds(2 * g, 2)
                def wide(v):
                    return v[:, ts].unsqueeze(2).to_broadcast([P, 2, D])
                ch.link(dve.tensor_tensor(xn[:], m.X[:, ts, :], wide(m.mean), ALU.subtract))
                ch.link(dve.tensor_tensor(xn[:], xn[:], wide(m.rstd), ALU.mult))
                ch.link(dve.tensor_tensor(m.X[:, ts, :], m.X[:, ts, :], xn[:], ALU.add))
                dve.wait_ge(s_y, ready(g))
                ch.link(dve.tensor_tensor(y[:], ps_y[b][:], b2[:].unsqueeze(1).to_broadcast([P, 2, D]), ALU.add))
                dve.sem_inc(s_fin, 1)
                ch.link(dve.tensor_tensor(y[:], y[:], wide(wts), ALU.mult))
                ch.link(dve.tensor_tensor(m.X[:, ts, :], m.X[:, ts, :], y[:], ALU.add))
            with dve.Fori(0, trips) as i:
                ch.loop(i, 12)
                finish(2 * i, 0)
                finish(2 * i + 1, 1)
            ch.end(trips)
            finish(2 * trips, 0)




TW = 8
NG = C1 // TW
FD = H1 * C1 * TW
FH = C1 * C1 // 2 - C1 * TW // 2
FO = H1 * FH
VW1 = C1 + 1
SCALE = float(C1) ** 0.25
KB_D, KB_O = FD // 128, FO // 128
NB = KB_D + KB_O


def head_of(blk):
    return blk // (KB_D // H1) if blk < KB_D else (blk - KB_D) // (KB_O // H1)


def products(ch, dve, feats, x):
    xg = x.rearrange("p (g i) -> p g i", i=TW)
    ch.step(dve.tensor_tensor(feats[:, 0:FD].rearrange("p (g i j) -> p g i j", i=TW, j=TW),
                              xg.unsqueeze(3).to_broadcast([P, H1 * NG, TW, TW]),
                              xg.unsqueeze(2).to_broadcast([P, H1 * NG, TW, TW]), ALU.mult))
    xh = x.rearrange("p (h i) -> p h i", h=H1)
    across = feats[:, FD:].rearrange("p (h f) -> p h f", h=H1)
    lo = 0
    for g in range(NG - 1):
        n = C1 - (g + 1) * TW
        ch.step(dve.tensor_tensor(across[:, :, lo:lo + TW * n].rearrange("p h (i j) -> p h i j", i=TW),
                                  xh[:, :, g * TW:(g + 1) * TW].unsqueeze(3).to_broadcast([P, H1, TW, n]),
                                  xh[:, :, (g + 1) * TW:].unsqueeze(2).to_broadcast([P, H1, TW, n]), ALU.mult))
        lo += TW * n


def normalise(ch, dve, out, x, sq, n2, rn, s_n, s_rn, t, factor, scale, gain=None):
    def by_head(v):
        return v.rearrange("p (h c) -> p h c", h=H1)
    ch.link(dve.tensor_tensor(sq, x, x, ALU.mult))
    ch.link(dve.tensor_reduce(n2, by_head(sq), AX.X, ALU.add))
    dve.tensor_scalar(n2, n2, scale * scale, 1e-24, ALU.mult, ALU.max).then_inc(s_n, 1)
    dve.wait_ge(s_rn, t + 1)
    if gain is not None:
        ch.link(dve.tensor_tensor(rn, rn, gain, ALU.mult))
    ch.link(dve.scalar_tensor_tensor(by_head(out), by_head(x), scale * factor,
                                     rn.unsqueeze(2).to_broadcast([P, H1, C1]), ALU.mult, ALU.mult))


@phase
def attention_sums(nc, m, tag, wkv, bkv, quad, lin, const):
    s_xn, s_pT, s_xT, s_kv, s_v, s_n, s_rn, s_f, s_mm, s_z = (
        m.sem(f"{tag}_{n}") for n in ("xn", "pT", "xT", "kv", "v", "n", "rn", "f", "mm", "z"))
    c_dve, c_act = m.sem(f"{tag}_dve"), m.sem(f"{tag}_act")
    s_cp, s_tr, s_row, s_bc = (m.sem(f"{tag}_{n}") for n in ("cp", "tr", "row", "bc"))
    HR = 64
    PR = H1 // 2
    RW = HR + VW1
    QD = FD // H1
    AW = FH + C1 + 1
    with ExitStack() as st:
        def sb(name, shape, dt=F32):
            return st.enter_context(nc.sbuf_tensor(f"{tag}_{name}", shape, dt))
        xn = [sb(f"xn{b}", [P, D]) for b in range(2)]
        xT = [sb(f"xT{b}", [128, 2, P]) for b in range(2)]
        kn = [sb(f"kn{b}", [P, D]) for b in range(2)]
        sq, n2, rn = sb("sq", [P, D]), sb("n2", [P, H1]), sb("rn", [P, H1])
        k = sb("k", [P, D])
        v1 = [sb(f"v1{b}", [P, H1, VW1]) for b in range(2)]
        feats = [sb(f"feats{b}", [P, FD + H1 * AW]) for b in range(2)]
        across = [feats[b][:, FD:].rearrange("p (h f) -> p h f", h=H1) for b in range(2)]
        sums_w, sums_a = sb("sums_w", [RW, PR, QD]), sb("sums_a", [RW, PR, AW])
        row = sb("row", [1, H1, VW1])
        zero = sb("zero", [P, 512])
        ps_t = st.enter_context(nc.psum_tensor(f"{tag}_pt", [128, 512], F32))
        ps_w = st.enter_context(nc.psum_tensor(f"{tag}_pw", [P, 512], F32))
        ps_s = [st.enter_context(nc.psum_tensor(f"{tag}_ps{j}", [128, 512], F32)) for j in range(PR // 2 + PR)]
        ps_d, ps_a = ps_s[0:PR // 2], ps_s[PR // 2:]
        block = st.enter_context(nc.Block())

        @block.vector
        def _(dve):
            ch = Chain(dve, c_dve)
            dve.memset(zero[:], 0.0).then_inc(s_z, 1)
            for b in range(2):
                dve.memset(v1[b][:], 1.0).then_inc(s_z, 1)
                dve.memset(across[b][:, :, AW - 1:AW], 1.0).then_inc(s_z, 1)
            dve.wait_ge(s_z, 5)

            def normed(t, b):
                dve.wait_ge(s_pT, free(t))
                dve.tensor_scalar(xn[b][:], m.X[:, t, :], m.mean[:, bass.ds(t, 1)], m.rstd[:, bass.ds(t, 1)],
                                  ALU.subtract, ALU.mult).then_inc(s_xn, 1)

            def features(t, b, more=True):
                dve.wait_ge(s_kv, t + 1)
                dve.wait_ge(s_mm, free(t))
                ch.step(dve.tensor_tensor(k[:], ps_w[:, 0:D], bkv[:, 0:D], ALU.add))
                ch.link(dve.tensor_tensor(v1[b][:, :, 1:VW1], ps_w[:, D:2 * D].rearrange("p (h c) -> p h c", h=H1),
                                          bkv[:, D:2 * D].rearrange("p (h c) -> p h c", h=H1), ALU.add))
                dve.sem_inc(s_v, 1)
                normalise(ch, dve, kn[b][:], k[:], sq[:], n2[:], rn[:], s_n, s_rn, t, SCALE, 1.0)
                if more:
                    normed(t + 1, 1 - b)
                ch.step(dve.tensor_copy(across[b][:, :, FH:FH + C1], kn[b].rearrange("p (h c) -> p h c", h=H1)))
                products(ch, dve, feats[b], kn[b][:])
                ch.settle()
                dve.sem_inc(s_f, 1)
            normed(0, 0)
            with dve.Fori(0, NT // 2 - 1) as i:
                ch.loop(i, 2 * (2 + 3 + 5))
                features(2 * i, 0)
                features(2 * i + 1, 1)
            ch.end(NT // 2 - 1)
            features(NT - 2, 0)
            features(NT - 1, 1, more=False)
            dve.wait_ge(s_mm, DEPTH + NT + 1)
            for j in range(PR // 2):
                dve.tensor_copy(sums_w[:, 2 * j:2 * j + 2, :], ps_d[j][0:RW, :].rearrange("p (j f) -> p j f", j=2)
                                ).then_inc(s_cp, 1)
            for j in range(PR):
                dve.tensor_copy(sums_a[:, j, :], ps_a[j][0:RW, 0:AW]).then_inc(s_cp, 1)
            dve.memset(lin[:], 0.0).then_inc(s_z, 1)
            dve.wait_ge(s_tr, 1)
            dve.wait_ge(s_z, 6)
            for h in range(H1):
                p_, e_ = h // 2, h % 2
                for blk, slot, c in ([(2 * h + c, c, 0.5 / N) for c in range(2)] +
                                     [(KB_D + 3 * h + c, 2 + c, 1.0 / N) for c in range(3)]):
                    n = p_ * 5 + slot
                    dve.tensor_scalar(quad[:, blk, :], ps_s[n // 4][:, n % 4 * 128 + e_ * HR:n % 4 * 128 + e_ * HR + VW1],
                                      c, None, ALU.mult)
                a_, r = h // 4, (h % 4) * C1
                dve.tensor_scalar(lin[r:r + C1, a_, h * VW1:(h + 1) * VW1],
                                  ps_t[r:r + C1, a_ * 128 + e_ * HR:a_ * 128 + e_ * HR + VW1], SCALE ** 2 / N, None,
                                  ALU.mult)
                dve.tensor_copy(row[:, h, :], ps_w[0:1, p_ * 128 + e_ * HR:p_ * 128 + e_ * HR + VW1]).then_inc(s_row, 1)
            dve.wait_ge(s_bc, 1)
            dve.tensor_scalar(const[:], ps_s[5][0:P, 0:H1 * VW1], SCALE ** 4 / N, None, ALU.mult)

        @block.scalar
        def _(act):
            ch = Chain(act, c_act)
            act.preload_act_table_set(NLE)
            with act.Fori(0, NT // 2) as i:
                ch.loop(i, 2)
                for b in range(2):
                    t = 2 * i + b
                    act.wait_ge(s_kv, t)
                    act.wait_ge(s_pT, ready(t))
                    act.sem_inc(m.s_pass, 1)
                    act.activation(xT[b][:].rearrange("p k n -> p (k n)"), ps_t[:, 0:2 * P], ACT.Copy).then_inc(s_xT, 1)
                    act.wait_ge(s_n, t + 1)
                    act.sem_inc(m.s_pass, 1)
                    ch.link(act.activation(rn[:], n2[:], ACT.Ln))
                    act.activation(rn[:], rn[:], ACT.Exp, scale=-0.5).then_inc(s_rn, 1)
            ch.end(NT // 2)

        @block.tensor
        def _(pe):
            pe.sem_inc(s_pT, DEPTH)
            pe.sem_inc(s_mm, DEPTH)
            pe.wait_ge(s_z, 5)
            for bank in ps_s:
                pe.matmul(bank[:, 0:512], zero[:, 0:128], zero[:], start=True, stop=False, skip_group_check=True)

            def keys(t, b):
                pe.wait_ge(s_xT, t)
                pe.wait_ge(s_xn, t + 1)
                pe.sem_inc(m.s_pass, 1)
                for k_ in range(2):
                    mm = pe.transpose(ps_t[:, k_ * P:(k_ + 1) * P], xn[b][:, k_ * 128:(k_ + 1) * 128], m.ident[0:P, 0:P])
                mm.then_inc(s_pT, 1)
                pe.wait_ge(s_v, t)
                pe.wait_ge(s_xT, t + 1)
                pe.sem_inc(m.s_pass, 1)
                for k_ in range(2):
                    mm = pe.matmul(ps_w[:], xT[b][:, k_, :], wkv[:, k_, :], start=(k_ == 0), stop=(k_ == 1))
                mm.then_inc(s_kv, 1)

            def sums(t, b):
                def add(to, w, x):
                    return pe.matmul(to, w, x, start=False, stop=False, skip_group_check=True)
                pe.wait_ge(s_f, t + 1)
                pe.sem_inc(m.s_pass, 1)
                for h in range(H1):
                    rows = slice(h % 2 * HR, h % 2 * HR + VW1)
                    j, lo = h // 4, h // 2 % 2 * QD
                    add(ps_d[j][rows, lo:lo + QD], v1[b][:, h, :], feats[b][:, h * QD:(h + 1) * QD])
                    mm = add(ps_a[h // 2][rows, 0:AW], v1[b][:, h, :], across[b][:, h, :])
                mm.then_inc(s_mm, 1)
            keys(0, 0)
            with pe.Fori(0, NT // 2 - 1) as i:
                keys(2 * i + 1, 1)
                sums(2 * i, 0)
                keys(2 * i + 2, 0)
                sums(2 * i + 1, 1)
            keys(NT - 1, 1)
            sums(NT - 2, 0)
            sums(NT - 1, 1)
            for bank in ps_s:
                mm = pe.matmul(bank[:, 0:512], zero[:, 0:128], zero[:], start=False, stop=True, skip_group_check=True)
            mm.then_inc(s_mm, 1)
            pe.wait_ge(s_cp, PR // 2 + PR)
            pe.wait_ge(s_rn, NT)
            ident = m.ident[0:RW, 0:RW]
            for p_ in range(PR):
                for slot in range(5):
                    n = p_ * 5 + slot
                    x = (sums_w[:, p_, slot * 128:(slot + 1) * 128] if slot < 2 else
                         sums_a[:, p_, (slot - 2) * 128:(slot - 1) * 128])
                    pe.transpose(ps_s[n // 4][:, n % 4 * 128:n % 4 * 128 + RW], x, ident)
                mm = pe.transpose(ps_w[0:1, p_ * 128:p_ * 128 + RW], sums_a[:, p_, AW - 1:AW], ident)
            for h in range(H1):
                a_, r = h // 4, (h % 4) * C1
                mm = pe.matmul(ps_t[r:r + C1, a_ * 128:a_ * 128 + RW], sums_a[:, h // 2, FH:FH + C1], ident, start=True,
                               stop=True)
            mm.then_inc(s_tr, 1)
            pe.wait_ge(s_row, H1)
            pe.matmul(ps_s[5][0:P, 0:H1 * VW1], m.ones[0:1, 0:P], row.rearrange("a h w -> a (h w)"), start=True,
                      stop=True).then_inc(s_bc, 1)


@phase
def attention_rows(nc, m, tag, wq, bq, gain, quad, lin, const, wproj, bproj):
    s_xn, s_pT, s_xT, s_q, s_qb, s_n, s_rn, s_f, s_gt, s_ge, s_y, s_o, s_po, s_oT, s_fT, s_r, s_fin = (
        m.sem(f"{tag}_{n}") for n in ("xn", "pT", "xT", "q", "qb", "n", "rn", "f", "gt", "ge", "y", "o", "po", "oT", "fT",
                                      "r", "fin"))
    c_dve, c_act = m.sem(f"{tag}_dve"), m.sem(f"{tag}_act")
    per = 4
    fills = NB // per + 1
    with ExitStack() as st:
        def sb(name, shape, dt=F32):
            return st.enter_context(nc.sbuf_tensor(f"{tag}_{name}", shape, dt))
        xn = [sb(f"xn{b}", [P, D]) for b in range(2)]
        xT = [sb(f"xT{b}", [128, 2, P]) for b in range(2)]
        q, sq, n2, rn = sb("q", [P, D]), sb("sq", [P, D]), sb("n2", [P, H1]), sb("rn", [P, H1])
        qn = [sb(f"qn{b}", [P, D]) for b in range(2)]
        feats = [sb(f"feats{b}", [P, FD + FO]) for b in range(2)]
        fT = [sb(f"fT{b}", [128, per, P]) for b in range(2)]
        y, r = sb("y", [P, H1, VW1]), sb("r", [P, H1])
        o = sb("o", [P, H1, C1])
        oT = sb("oT", [128, 2, P])
        ps_t = st.enter_context(nc.psum_tensor(f"{tag}_pt", [128, 512], F32))
        ps_w = st.enter_context(nc.psum_tensor(f"{tag}_pw", [P, 512], F32))
        ps_f = [st.enter_context(nc.psum_tensor(f"{tag}_pf{b}", [128, 512], F32)) for b in range(2)]
        ps_y = st.enter_context(nc.psum_tensor(f"{tag}_py", [P, 512], F32))
        ps_r = st.enter_context(nc.psum_tensor(f"{tag}_pr", [P, 512], F32))
        ps_o = st.enter_context(nc.psum_tensor(f"{tag}_po", [128, 512], F32))
        block = st.enter_context(nc.Block())

        @block.vector
        def _(dve):
            ch = Chain(dve, c_dve)

            def normed(t, b):
                dve.wait_ge(s_pT, free(t))
                dve.tensor_scalar(xn[b][:], m.X[:, t, :], m.mean[:, bass.ds(t, 1)], m.rstd[:, bass.ds(t, 1)],
                                  ALU.subtract, ALU.mult).then_inc(s_xn, 1)

            def features(t, b, more=True):
                dve.wait_ge(s_q, t + 1)
                dve.wait_ge(s_y, free(t))
                ch.link(dve.tensor_tensor(q[:], ps_w[:, 0:D], bq[:], ALU.add))
                dve.sem_inc(s_qb, 1)
                normalise(ch, dve, qn[b][:], q[:], sq[:], n2[:], rn[:], s_n, s_rn, t, SCALE, SCALE, gain[:])
                if more:
                    normed(t + 1, 1 - b)
                products(ch, dve, feats[b], qn[b][:])
                ch.settle()
                dve.sem_inc(s_f, 1)

            def quotients(t):
                dve.wait_ge(s_y, ready(t))
                ch.link(dve.tensor_tensor(y.rearrange("p h w -> p (h w)"), ps_y[:, 0:H1 * VW1], const[:], ALU.add))
                ch.link(dve.reciprocal(r[:], y[:, :, 0]))
                dve.wait_ge(s_po, t)
                ch.link(dve.tensor_tensor(o[:], y[:, :, 1:VW1], r[:].unsqueeze(2).to_broadcast([P, H1, C1]), ALU.mult))
                dve.sem_inc(s_o, 1)

            def rows(t):
                ch.link(dve.tensor_tensor(m.X[:, t, :], m.X[:, t, :], bproj[:], ALU.add))
                dve.wait_ge(s_r, t + 1)
                ch.link(dve.tensor_tensor(m.X[:, t, :], m.X[:, t, :], ps_r[:, 0:D], ALU.add))
                dve.sem_inc(s_fin, 1)
            normed(0, 0)
            features(0, 0)
            features(1, 1)
            quotients(0)
            with dve.Fori(0, NT // 2 - 2) as i:
                ch.loop(i, 2 * (1 + 4 + 4 + 5))
                for b in range(2):
                    t = 2 * i + b
                    features(t + 2, b)
                    rows(t)
                    quotients(t + 1)
            ch.end(NT // 2 - 2)
            for b in range(2):
                t = NT - 4 + b
                features(t + 2, b, more=(b == 0))
                rows(t)
                quotients(t + 1)
            rows(NT - 2)
            quotients(NT - 1)
            rows(NT - 1)

        MIDDLE = fills // 2

        @block.scalar
        def _(act):
            ch = Chain(act, c_act)
            act.preload_act_table_set(NLE)

            def rows_T(t, b):
                act.wait_ge(s_q, t)
                act.wait_ge(s_pT, ready(t))
                act.sem_inc(m.s_pass, 1)
                act.activation(xT[b][:].rearrange("p k n -> p (k n)"), ps_t[:, 0:2 * P], ACT.Copy).then_inc(s_xT, 1)

            def norms(t):
                act.wait_ge(s_n, t + 1)
                act.sem_inc(m.s_pass, 1)
                ch.link(act.activation(rn[:], n2[:], ACT.Ln))
                act.activation(rn[:], rn[:], ACT.Exp, scale=-0.5).then_inc(s_rn, 1)

            def outputs(t):
                act.wait_ge(s_po, t + 1)
                act.wait_ge(s_r, t)
                act.sem_inc(m.s_pass, 1)
                act.activation(oT[:].rearrange("p k n -> p (k n)"), ps_o[:, 0:2 * P], ACT.Copy).then_inc(s_oT, 1)

            def tile(t, b, before=True, after=True):
                if after:
                    rows_T(t + 1, 1 - b)
                for f in range(fills):
                    n = t * fills + f
                    c = per if f else 2
                    act.wait_ge(s_ge, n + 1)
                    act.wait_ge(s_gt, n + 1)
                    act.sem_inc(m.s_pass, 1)
                    act.activation(fT[(b * fills + f) % 2][:, 0:c, :].rearrange("p k n -> p (k n)"),
                                   ps_f[(b * fills + f) % 2][:, 0:c * P], ACT.Copy).then_inc(s_fT, 1)
                    if f == 1 and after:
                        norms(t + 1)
                    if f == MIDDLE and before:
                        outputs(t - 1)
            rows_T(0, 0)
            norms(0)
            tile(0, 0, before=False)
            with act.Fori(0, NT // 2 - 1) as i:
                ch.loop(i, 2)
                tile(2 * i + 1, 1)
                tile(2 * i + 2, 0)
            ch.end(NT // 2 - 1)
            tile(NT - 1, 1, after=False)
            outputs(NT - 1)

        @block.tensor
        def _(pe):
            pe.sem_inc(s_pT, DEPTH)
            pe.sem_inc(s_y, DEPTH)
            pe.sem_inc(s_ge, DEPTH)

            def queries(t, b):
                pe.wait_ge(s_xT, t)
                pe.wait_ge(s_xn, t + 1)
                pe.sem_inc(m.s_pass, 1)
                for k_ in range(2):
                    mm = pe.transpose(ps_t[:, k_ * P:(k_ + 1) * P], xn[b][:, k_ * 128:(k_ + 1) * 128],
                                      m.ident[0:P, 0:P])
                mm.then_inc(s_pT, 1)
                pe.wait_ge(s_qb, t)
                pe.wait_ge(s_xT, t + 1)
                pe.sem_inc(m.s_pass, 1)
                for k_ in range(2):
                    mm = pe.matmul(ps_w[:, 0:D], xT[b][:, k_, :], wq[:, k_, :], start=(k_ == 0), stop=(k_ == 1))
                mm.then_inc(s_q, 1)

            def transposes(t, b, f):
                j = (b * fills + f) % 2
                if f:
                    blocks = [feats[b][:, x * 128:(x + 1) * 128] for x in range((f - 1) * per, f * per)]
                else:
                    blocks = [qn[b][:, x * 128:(x + 1) * 128] for x in range(2)]
                for c, x in enumerate(blocks):
                    mm = pe.transpose(ps_f[j][:, c * P:(c + 1) * P], x, m.ident[0:P, 0:P])
                mm.then_inc(s_gt, 1)

            def sums(t, b, f):
                j = (b * fills + f) % 2
                pe.wait_ge(s_fT, t * fills + f + 1)
                pe.sem_inc(m.s_pass, 1)
                if f == 0:
                    for a in range(2):
                        mm = pe.matmul(ps_y[:, 0:H1 * VW1], fT[j][:, a, :], lin[:, a, :], start=(a == 0),
                                       stop=False, skip_group_check=True)
                else:
                    for c in range(per):
                        blk = (f - 1) * per + c
                        h = head_of(blk)
                        mm = pe.matmul(ps_y[:, h * VW1:(h + 1) * VW1], fT[j][:, c, :], quad[:, blk, :],
                                       start=False, stop=(f == fills - 1 and c == per - 1),
                                       skip_group_check=True)
                mm.then_inc(s_ge, 1)

            def outputs_T(t):
                pe.wait_ge(s_o, t + 1)
                pe.sem_inc(m.s_pass, 1)
                for k_ in range(2):
                    mm = pe.transpose(ps_o[:, k_ * P:(k_ + 1) * P],
                                      o.rearrange("p h c -> p (h c)")[:, k_ * 128:(k_ + 1) * 128], m.ident[0:P, 0:P])
                mm.then_inc(s_po, 1)

            def outputs(t):
                pe.wait_ge(s_fin, t)
                pe.wait_ge(s_oT, t + 1)
                pe.sem_inc(m.s_pass, 1)
                for k_ in range(2):
                    mm = pe.matmul(ps_r[:, 0:D], oT[:, k_, :], wproj[:, k_, :], start=(k_ == 0), stop=(k_ == 1))
                mm.then_inc(s_r, 1)

            def tile(t, b, before=True, after=True):
                if after:
                    queries(t + 1, 1 - b)
                pe.wait_ge(s_f, t + 1)
                pe.sem_inc(m.s_pass, 1)
                transposes(t, b, 0)
                transposes(t, b, 1)
                pe.wait_ge(s_o, t)
                for f in range(fills):
                    sums(t, b, f)
                    if f + 2 < fills:
                        transposes(t, b, f + 2)
                    if f == MIDDLE - 1 and before:
                        outputs_T(t - 1)
                    if f == MIDDLE + 1 and before:
                        outputs(t - 1)
                pe.wait_ge(s_ge, DEPTH + (t + 1) * fills)
                pe.sem_inc(s_y, 1)
            queries(0, 0)
            tile(0, 0, before=False)
            with pe.Fori(0, NT // 2 - 1) as i:
                tile(2 * i + 1, 1)
                tile(2 * i + 2, 0)
            tile(NT - 1, 1, after=False)
            outputs_T(NT - 1)
            outputs(NT - 1)



HS, CS = 8, 64
WS = HS * CS
SB = WS // 128


@phase
def fold_slices(nc, m, tag, wx, bx, wsl, bsl, temp, wlg, blg):
    s_t, s_c, s_mm, s_v = (m.sem(f"{tag}_{n}") for n in ("t", "c", "mm", "v"))
    with ExitStack() as st:
        wxT = st.enter_context(nc.sbuf_tensor(f"{tag}_wxT", [CS, 2, HS, 128], F32))
        bxb = st.enter_context(nc.sbuf_tensor(f"{tag}_bxb", [CS, HS, P], F32))
        ps_t = st.enter_context(nc.psum_tensor(f"{tag}_pt", [128, 2, HS, 128], F32))
        ps_w = st.enter_context(nc.psum_tensor(f"{tag}_pw", [128, 2, HS, CS], F32))
        ps_b = st.enter_context(nc.psum_tensor(f"{tag}_pb", [P, HS, CS], F32))
        block = st.enter_context(nc.Block())

        @block.tensor
        def _(pe):
            for k in range(2):
                for h in range(HS):
                    mm = pe.transpose(ps_t[0:CS, k, h, :], wx[:, k, h * CS:(h + 1) * CS], m.ident[:])
            mm.then_inc(s_t, 1)
            pe.wait_ge(s_c, 2)
            for h in range(HS):
                for k in range(2):
                    pe.matmul(ps_w[:, k, h, :], wxT[:, k, h, :], wsl[:], start=True, stop=True)
                mm = pe.matmul(ps_b[:, h, :], bxb[:, h, :], wsl[:], start=True, stop=True)
            mm.then_inc(s_mm, 1)

        @block.vector
        def _(dve):
            dve.tensor_scalar(temp[:], temp[:], 0.1, 5.0, ALU.max, ALU.min).then_inc(s_v, 1)
            dve.tensor_tensor(bxb[:], m.ones[0:CS, 0:P].unsqueeze(1).to_broadcast([CS, HS, P]),
                              bx[:].unsqueeze(2).to_broadcast([CS, HS, P]), ALU.mult).then_inc(s_c, 1)
            dve.wait_ge(s_t, 1)
            dve.tensor_copy(wxT[:], ps_t[0:CS]).then_inc(s_c, 1)
            dve.wait_ge(s_v, 1)
            dve.reciprocal(temp[:], temp[:]).then_inc(s_v, 1)
            dve.wait_ge(s_mm, 1)
            dve.tensor_tensor(blg.rearrange("p (h g) -> p h g", h=HS), ps_b[:],
                              bsl[:].unsqueeze(1).to_broadcast([P, HS, CS]), ALU.add).then_inc(s_v, 1)
            dve.wait_ge(s_v, 3)
            for k in range(2):
                dve.tensor_tensor(wlg[:, k, :].rearrange("p (h g) -> p h g", h=HS), ps_w[:, k],
                                  temp[:].unsqueeze(2).to_broadcast([128, HS, CS]), ALU.mult)
            dve.tensor_tensor(blg.rearrange("p (h g) -> p h g", h=HS), blg.rearrange("p (h g) -> p h g", h=HS),
                              temp[0:P, :].unsqueeze(2).to_broadcast([P, HS, CS]), ALU.mult)


@phase
def slice_sums(nc, m, tag, wlg, blg, wT_all, sums):
    s_xn, s_pT, s_xT, s_lg, s_p1, s_e, s_p2, s_pw, s_wT, s_ws, s_z = (
        m.sem(f"{tag}_{n}") for n in ("xn", "pT", "xT", "lg", "p1", "e", "p2", "pw", "wT", "ws", "z"))
    c_dve = m.sem(f"{tag}_dve")
    with ExitStack() as st:
        def sb(name, shape, dt=F32):
            return st.enter_context(nc.sbuf_tensor(f"{tag}_{name}", shape, dt))
        xa = [sb(f"xa{j}", [P, D + 1]) for j in range(4)]
        xT = [sb(f"xT{b}", [128, 2, P]) for b in range(2)]
        w = [sb(f"w{j}", [P, HS, CS]) for j in range(4)]
        mx, den = sb("mx", [P, HS]), sb("den", [P, HS])
        zero = sb("zero", [P, 512])
        ps_t = st.enter_context(nc.psum_tensor(f"{tag}_pt", [128, 512], F32))
        ps_w = [st.enter_context(nc.psum_tensor(f"{tag}_pw{b}", [P, 512], F32)) for b in range(2)]
        ps_wT = st.enter_context(nc.psum_tensor(f"{tag}_pwT", [128, 512], F32))
        ps_s = [st.enter_context(nc.psum_tensor(f"{tag}_ps{j}", [128, 512], F32)) for j in range(SB)]
        block = st.enter_context(nc.Block())

        @block.vector
        def _(dve):
            ch = Chain(dve, c_dve)
            dve.sem_inc(s_p1, DEPTH)
            dve.memset(zero[:], 0.0).then_inc(s_z, 1)
            for j in range(4):
                dve.memset(xa[j][:, D:D + 1], 1.0).then_inc(s_z, 1)

            def normed(t, j):
                dve.wait_ge(s_ws, t + 1)
                dve.tensor_scalar(xa[j][:, 0:D], m.X[:, t, :], m.mean[:, bass.ds(t, 1)], m.rstd[:, bass.ds(t, 1)],
                                  ALU.subtract, ALU.mult).then_inc(s_xn, 1)

            def shifted(t, j):
                dve.wait_ge(s_lg, t + 2)
                ch.link(dve.tensor_tensor(w[j].rearrange("p h g -> p (h g)"), ps_w[j % 2][:], blg[:], ALU.add))
                ch.link(dve.tensor_reduce(mx[:], w[j][:], AX.X, ALU.max))
                dve.tensor_tensor(w[j][:], w[j][:], mx[:].unsqueeze(2).to_broadcast([P, HS, CS]), ALU.subtract
                                  ).then_inc(s_p1, 1)

            def divided(t, j):
                dve.wait_ge(s_e, t + 1)
                ch.link(dve.tensor_reduce(den[:], w[j][:], AX.X, ALU.add))
                ch.link(dve.reciprocal(den[:], den[:]))
                dve.tensor_tensor(w[j][:], w[j][:], den[:].unsqueeze(2).to_broadcast([P, HS, CS]), ALU.mult
                                  ).then_inc(s_p2, 1)
                dve.wait_ge(s_p2, t + 1)

            def tile(t, j):
                shifted(t + 1, (j + 1) % 4)
                if not isinstance(t, int) or t + 3 < NT:
                    normed(t + 3, (j + 3) % 4)
                divided(t + 1, (j + 1) % 4)
            for t in range(3):
                normed(t, t)
            shifted(0, 0)
            divided(0, 0)
            trips = (NT - 3) // 4
            with dve.Fori(0, trips) as i:
                ch.loop(i, 16)
                for j in range(4):
                    tile(4 * i + j, j)
            ch.end(trips)
            for t in range(4 * trips, NT - 1):
                tile(t, t % 4)
            dve.wait_ge(s_ws, 4 + NT + 1)
            for j in range(SB):
                dve.tensor_copy(sums[:, j, :], ps_s[j][:, 0:D + 1])

        @block.scalar
        def _(act):
            def rows_T(t, b):
                act.wait_ge(s_pT, t + 1)
                act.wait_ge(s_lg, t)
                act.sem_inc(m.s_pass, 1)
                act.activation(xT[b].rearrange("p k n -> p (k n)"), ps_t[:, 0:2 * P], ACT.Copy).then_inc(s_xT, 1)

            def powers(t, j):
                act.wait_ge(s_p1, ready(t))
                act.sem_inc(m.s_pass, 1)
                act.activation(w[j][:], w[j][:], ACT.Exp).then_inc(s_e, 1)

            def tile(t, j, n=2):
                if n == 2:
                    rows_T(t + 2, j % 2)
                if n >= 1:
                    powers(t + 1, (j + 1) % 4)
                act.wait_ge(s_pw, t + 1)
                act.sem_inc(m.s_pass, 1)
                act.activation(wT_all[:, t, :], ps_wT[:, 0:SB * P], ACT.Copy).then_inc(s_wT, 1)
            rows_T(0, 0)
            rows_T(1, 1)
            powers(0, 0)
            with act.Fori(0, NT // 4) as i:
                for j in range(4):
                    tile(4 * i + j, j)
            tile(NT - 2, 0, 1)
            tile(NT - 1, 1, 0)

        @block.tensor
        def _(pe):
            pe.sem_inc(s_ws, 4)
            pe.sem_inc(s_lg, 1)
            pe.wait_ge(s_z, 5)
            for bank in ps_s:
                pe.matmul(bank[:, 0:D + 1], zero[:, 0:128], zero[:, 0:D + 1], start=True, stop=False,
                          skip_group_check=True)

            def transposes(t, j):
                pe.wait_ge(s_xT, t)
                pe.wait_ge(s_xn, t + 1)
                pe.sem_inc(m.s_pass, 1)
                for k in range(2):
                    mm = pe.transpose(ps_t[:, k * P:(k + 1) * P], xa[j][:, k * 128:(k + 1) * 128], m.ident[0:P, 0:P])
                mm.then_inc(s_pT, 1)

            def logits(t, j):
                pe.wait_ge(s_xT, t + 1)
                pe.wait_ge(s_p1, free(t))
                pe.sem_inc(m.s_pass, 1)
                for k in range(2):
                    mm = pe.matmul(ps_w[j % 2][:], xT[j % 2][:, k, :], wlg[:, k, :], start=(k == 0), stop=(k == 1))
                mm.then_inc(s_lg, 1)

            def tile(t, j, n=2):
                if n == 2:
                    transposes(t + 2, (j + 2) % 4)
                if n >= 1:
                    logits(t + 1, (j + 1) % 4)
                pe.wait_ge(s_wT, t)
                pe.wait_ge(s_p2, t + 1)
                pe.sem_inc(m.s_pass, 1)
                wf = w[j].rearrange("p h g -> p (h g)")
                for c in range(SB):
                    mm = pe.transpose(ps_wT[:, c * P:(c + 1) * P], wf[:, c * 128:(c + 1) * 128], m.ident[0:P, 0:P])
                mm.then_inc(s_pw, 1)
                for c in range(SB):
                    mm = pe.matmul(ps_s[c][:, 0:D + 1], wf[:, c * 128:(c + 1) * 128], xa[j][:], start=False,
                                   stop=False, skip_group_check=True)
                mm.then_inc(s_ws, 1)
            transposes(0, 0)
            transposes(1, 1)
            logits(0, 0)
            with pe.Fori(0, NT // 4) as i:
                for j in range(4):
                    tile(4 * i + j, j)
            tile(NT - 2, 0, 1)
            tile(NT - 1, 1, 0)
            for bank in ps_s:
                mm = pe.matmul(bank[:, 0:D + 1], zero[:, 0:128], zero[:, 0:D + 1], start=False, stop=True,
                               skip_group_check=True)
            mm.then_inc(s_ws, 1)


@phase
def slice_attention(nc, m, tag, sums, wfx, bfx, wq, wk, wv, wout, rows):
    s_pe, s_v, s_e = (m.sem(f"{tag}_{n}") for n in ("pe", "v", "e"))
    c_dve = m.sem(f"{tag}_dve")
    with ExitStack() as st:
        def sb(name, shape, dt=F32):
            return st.enter_context(nc.sbuf_tensor(f"{tag}_{name}", shape, dt))
        sT, nrow = sb("sT", [128, 2, WS]), sb("nrow", [1, WS])
        tok, tokT, qT, kT, v, att, attT, osT = (sb(n, [CS, WS]) for n in
                                                ("tok", "tokT", "qT", "kT", "v", "att", "attT", "osT"))
        rn, mx, den = (sb(n, [CS, HS]) for n in ("rn", "mx", "den"))
        ps_a = st.enter_context(nc.psum_tensor(f"{tag}_pa", [128, 2, 512], F32))
        ps_b = st.enter_context(nc.psum_tensor(f"{tag}_pb", [128, 512], F32))
        ps_c = st.enter_context(nc.psum_tensor(f"{tag}_pc", [128, 512], F32))
        ps_p = st.enter_context(nc.psum_tensor(f"{tag}_pp", [128, HS, D], F32))
        block = st.enter_context(nc.Block())

        def head(x, h):
            return x[:, h * CS:(h + 1) * CS]

        def by_head(x):
            return x.rearrange("p (h c) -> p h c", h=HS)

        def spread_(x):
            return x.unsqueeze(2).to_broadcast([CS, HS, CS])

        @block.tensor
        def _(pe):
            ident = m.ident[0:CS, 0:CS]
            for j in range(SB):
                for k in range(2):
                    pe.transpose(ps_a[:, k, j * 128:(j + 1) * 128], sums[:, j, k * 128:(k + 1) * 128], m.ident[:])
                mm = pe.transpose(ps_b[0:1, j * 128:(j + 1) * 128], sums[:, j, D:D + 1], m.ident[:])
            mm.then_inc(s_pe, 1)
            pe.wait_ge(s_v, 1)
            for h in range(HS):
                for k in range(2):
                    pe.matmul(head(ps_c[0:CS, :], h), head(sT[:, k, :], h), head(wfx[:, k, :], h), start=(k == 0),
                              stop=False)
                pe.matmul(head(ps_c[0:CS, :], h), head(nrow[:], h), head(bfx[:], h), start=False, stop=True)
                mm = pe.matmul(ps_p[0:CS, 0, h:h + 1], head(nrow[:], h), m.ones[0:1, 0:1], start=True, stop=True)
            mm.then_inc(s_pe, 1)
            pe.wait_ge(s_v, 2)
            for h in range(HS):
                mm = pe.transpose(head(ps_b[0:CS, :], h), head(tok[:], h), ident)
            mm.then_inc(s_pe, 1)
            pe.wait_ge(s_v, 3)
            pe.matmul(ps_a[0:CS, 0, :], wq[:], tokT[:], start=True, stop=True)
            pe.matmul(ps_a[0:CS, 1, :], wk[:], tokT[:], start=True, stop=True)
            for h in range(HS):
                mm = pe.matmul(head(ps_c[0:CS, :], h), head(tokT[:], h), wv[:], start=True, stop=True)
            mm.then_inc(s_pe, 1)
            pe.wait_ge(s_v, 4)
            for h in range(HS):
                mm = pe.matmul(head(ps_b[0:CS, :], h), head(qT[:], h), head(kT[:], h), start=True, stop=True)
            mm.then_inc(s_pe, 1)
            pe.wait_ge(s_v, 6)
            for h in range(HS):
                mm = pe.transpose(head(ps_c[0:CS, :], h), head(att[:], h), ident)
            mm.then_inc(s_pe, 1)
            pe.wait_ge(s_v, 7)
            for h in range(HS):
                mm = pe.matmul(head(ps_b[0:CS, :], h), head(v[:], h), head(attT[:], h), start=True, stop=True)
            mm.then_inc(s_pe, 1)
            pe.wait_ge(s_v, 8)
            for h in range(HS):
                mm = pe.matmul(ps_p[:, h, :], osT[:, h // 2 * 128:(h // 2 + 1) * 128], wout[:, h, :], start=True,
                               stop=True)
            mm.then_inc(s_pe, 1)

        @block.scalar
        def _(act):
            act.wait_ge(s_v, 5)
            act.activation(att[:], att[:], ACT.Exp, scale=CS ** -0.5).then_inc(s_e, 1)

        @block.vector
        def _(dve):
            ch = Chain(dve, c_dve)
            dve.wait_ge(s_pe, 1)
            ch.link(dve.tensor_copy(nrow[:], ps_b[0:1, :]))
            dve.tensor_copy(sT[:], ps_a[:]).then_inc(s_v, 1)
            dve.wait_ge(s_pe, 2)
            ch.link(dve.tensor_scalar(rn[:], ps_p[0:CS, 0, 0:HS], 1e-5, None, ALU.add))
            ch.link(dve.reciprocal(rn[:], rn[:]))
            dve.tensor_tensor(by_head(tok[:]), by_head(ps_c[0:CS, :]), spread_(rn[:]), ALU.mult).then_inc(s_v, 1)
            dve.wait_ge(s_pe, 3)
            dve.tensor_copy(tokT[:], ps_b[0:CS, :]).then_inc(s_v, 1)
            dve.wait_ge(s_pe, 4)
            ch.step(dve.tensor_copy(qT[:], ps_a[0:CS, 0, :]))
            ch.step(dve.tensor_copy(kT[:], ps_a[0:CS, 1, :]))
            ch.settle()
            dve.tensor_copy(v[:], ps_c[0:CS, :]).then_inc(s_v, 1)
            dve.wait_ge(s_pe, 5)
            ch.link(dve.tensor_reduce(mx[:], by_head(ps_b[0:CS, :]), AX.X, ALU.max))
            dve.tensor_tensor(by_head(att[:]), by_head(ps_b[0:CS, :]), spread_(mx[:]), ALU.subtract).then_inc(s_v, 1)
            dve.wait_ge(s_e, 1)
            ch.link(dve.tensor_reduce(den[:], by_head(att[:]), AX.X, ALU.add))
            ch.link(dve.reciprocal(den[:], den[:]))
            dve.tensor_tensor(by_head(att[:]), by_head(att[:]), spread_(den[:]), ALU.mult).then_inc(s_v, 1)
            dve.wait_ge(s_pe, 6)
            dve.tensor_copy(attT[:], ps_c[0:CS, :]).then_inc(s_v, 1)
            dve.wait_ge(s_pe, 7)
            dve.tensor_copy(osT[:], ps_b[0:CS, :]).then_inc(s_v, 1)
            dve.wait_ge(s_pe, 8)
            for e in range(2):
                lanes = slice(e * CS, (e + 1) * CS)
                dve.tensor_copy(rows[lanes], ps_p[lanes].rearrange("p (j e) d -> p j e d", e=2)[:, :, e, :])


@phase
def slice_rows(nc, m, tag, wT_all, rows, bout, out):
    s_c, s_mm, s_b, s_fin = (m.sem(f"{tag}_{n}") for n in ("c", "mm", "b", "fin"))
    s_out = m.sem(f"{tag}_out")
    out_v = out.rearrange("(t p) d -> t p d", p=P)
    with ExitStack() as st:
        wT = [st.enter_context(nc.sbuf_tensor(f"{tag}_wT{b}", [128, SB * P], F32)) for b in range(2)]
        ps_o = [st.enter_context(nc.psum_tensor(f"{tag}_po{b}", [P, 512], F32)) for b in range(2)]
        block = st.enter_context(nc.Block())

        @block.scalar
        def _(act):
            with act.Fori(0, NT // 2) as i:
                for b in range(2):
                    t = 2 * i + b
                    act.wait_ge(s_mm, free(t))
                    act.sem_inc(m.s_pass, 1)
                    act.activation(wT[b][:], wT_all[:, t, :], ACT.Copy).then_inc(s_c, 1)

        @block.tensor
        def _(pe):
            pe.sem_inc(s_mm, DEPTH)
            with pe.Fori(0, NT // 2) as i:
                for b in range(2):
                    t = 2 * i + b
                    pe.wait_ge(s_c, t + 1)
                    pe.wait_ge(s_fin, free(t))
                    pe.sem_inc(m.s_pass, 1)
                    for j in range(SB):
                        mm = pe.matmul(ps_o[b][:, 0:D], wT[b][:, j * P:(j + 1) * P], rows[:, j, :], start=(j == 0),
                                       stop=(j == SB - 1))
                    mm.then_inc(s_mm, 1)

        @block.vector
        def _(dve):
            dve.sem_inc(s_fin, DEPTH)
            with dve.Fori(0, NT // 2) as i:
                for b in range(2):
                    t = 2 * i + b
                    dve.tensor_tensor(m.X[:, t, :], m.X[:, t, :], bout[:], ALU.add).then_inc(s_b, 1)
                    dve.wait_ge(s_mm, ready(t))
                    dve.wait_ge(s_b, t + 1)
                    dve.sem_inc(m.s_pass, 1)
                    dve.tensor_tensor(m.X[:, t, :], m.X[:, t, :], ps_o[b][:, 0:D], ALU.add).then_inc(s_fin, 1)

        @block.sync
        def _(sp):
            with sp.Fori(0, NT) as t:
                sp.wait_ge(s_fin, ready(t))
                sp.dma_start(out_v[t], m.X[:, t, :]).then_inc(s_out, 16)
            sp.wait_ge(s_out, 16 * NT)


def feed1(nc, m, a, out):
    with ExitStack() as st:
        def sb(name, shape, dt=F32):
            return st.enter_context(nc.sbuf_tensor(name, shape, dt))
        wT_all = sb("wT_all", [128, NT, SB * P])
        rows, bout = sb("s_rows", [128, SB, D]), sb("s_bout", [P, D])
        with ExitStack() as st2:
            def sb2(name, shape, dt=F32):
                return st2.enter_context(nc.sbuf_tensor(name, shape, dt))
            sums = sb2("s_sums", [128, SB, D + 1])
            with ExitStack() as st3:
                def sb3(name, shape, dt=F32):
                    return st3.enter_context(nc.sbuf_tensor(name, shape, dt))
                wlg, blg = sb3("wlg", [128, 2, WS]), sb3("blg", [P, WS])
                wx, bx, wsl, bsl = sb3("wx", [128, 2, WS]), sb3("bx", [CS, HS]), sb3("wsl", [CS, CS]), sb3("bsl", [P, CS])
                temp = sb3("s_temp", [128, HS])
                load(nc, m, "w5", [(wx[:], kmaj(a["L1_ffn_W_x"])), (bx[:], a["L1_ffn_b_x"].rearrange("(h d) -> d h", h=HS)),
                                   (wsl[:], a["L1_ffn_W_slice"]), (bsl[:], bcast(a["L1_ffn_b_slice"], P)),
                                   (temp[:], bcast(a["L1_ffn_temperature"].rearrange("a h b c -> (a h b c)"), 128)),
                                   (bout[:], bcast(a["L1_ffn_b_out"], P))])
                norm_stats(nc, m, "ln3")
                fold_slices(nc, m, "fs", wx, bx, wsl, bsl, temp, wlg, blg)
                slice_sums(nc, m, "ss", wlg, blg, wT_all, sums)
            wfx, bfx = sb2("wfx", [128, 2, WS]), sb2("bfx", [1, WS])
            wq, wk, wv, wout = sb2("s_wq", [CS, CS]), sb2("s_wk", [CS, CS]), sb2("s_wv", [CS, CS]), sb2("s_wo", [CS, HS, D])
            load(nc, m, "w6", [(wfx[:], kmaj(a["L1_ffn_W_fx"])), (bfx[:], bcast(a["L1_ffn_b_fx"], 1)),
                               (wq[:], a["L1_ffn_W_q"]), (wk[:], a["L1_ffn_W_k"]), (wv[:], a["L1_ffn_W_v"]),
                               (wout[:], kmaj(a["L1_ffn_W_out"], CS))])
            slice_attention(nc, m, "sa", sums, wfx, bfx, wq, wk, wv, wout, rows)
        slice_rows(nc, m, "so", wT_all, rows, bout, out)


@phase
def load(nc, m, tag, pairs):
    s_ld = m.sem(f"{tag}_ld")
    with nc.Block() as block:
        @block.sync
        def _(sp):
            with nc.allow_non_contiguous_dma(reason="columns of weights"):
                for dst, src in pairs:
                    sp.dma_start(dst, src).then_inc(s_ld, 16)
            sp.wait_ge(s_ld, 16 * len(pairs))


def kmaj(ap, k=128):
    return ap.rearrange("(b k) n -> k b n", k=k)


def block0(nc, m, a):
    with ExitStack() as st:
        def sb(name, shape, dt=F32):
            return st.enter_context(nc.sbuf_tensor(name, shape, dt))
        m.fac = sb("fac", [P, NT])
        m.rfac = sb("rfac", [P, NT])
        wc = sb("wc", [128, 2, CV])
        bnb = sb("bnb", [P, CV])
        with ExitStack() as st2:
            def sb2(name, shape, dt=F32):
                return st2.enter_context(nc.sbuf_tensor(name, shape, dt))
            wlr = sb2("wlr", [128, 2, 2 * W0])
            blr = sb2("blr", [P, 2 * W0])
            gram = sb2("gram", [128, 2, D + 1])
            load(nc, m, "w0", [(wlr[:, :, 0:W0], kmaj(a["L0_gnn_Wl1"])), (wlr[:, :, W0:], kmaj(a["L0_gnn_Wr1"])),
                               (blr[:, 0:W0], bcast(a["L0_gnn_bl1"], P)), (blr[:, W0:], bcast(a["L0_gnn_br1"], P)),
                               (wc[:], kmaj(a["qkv_taps"][2]))])
            norm_stats(nc, m, "ln0", ball=True)
            node_tables(nc, m, "tb0", wlr, 2 * W0, W0, m.tl, m.tr, m.edge_rows, bias=blr, gram=gram)
            gamma, beta = sb2("gamma", [128, CV]), sb2("beta", [128, CV])
            load(nc, m, "bn", [(gamma[:], bcast(a["L0_mix_bn_gamma"], 128)), (beta[:], bcast(a["L0_mix_bn_beta"], 128))])
            fold_batch_norm(nc, m, wc, bnb, gram, gamma, beta)
        bd = sb("bd", [128, 6, 128])
        dwc = sb("dwc", [128, 6])
        res = sb("res", [128, 4, D])
        b_res = sb("b_res", [P, D])
        att = sb("att", [P, CB * W0])
        mixer = Mixer(nc, m, st, wc, bnb, bd, res, b_res)
        prepare_mixer(nc, m, a, mixer, bd, dwc, res, b_res, att)
        chunk_rows(nc, m, "cr0", m.tr, m.edge_rows)
        edge_layer(nc, m, "e0", H0, W0, m.tl, m.edge_rows, m.pieces0, att=att, mixer=mixer)
        with ExitStack() as st2:
            def sb2(name, shape, dt=F32):
                return st2.enter_context(nc.sbuf_tensor(name, shape, dt))
            bias1, bias2 = sb2("g_bias1", [P, W0]), sb2("g_bias2", [P, W0])
            wlr2, blr2 = sb2("wlr2", [W0, 2 * W0]), sb2("blr2", [P, 2 * W0])
            wo, bo = sb2("wo", [W0, D]), sb2("bo", [P, D])
            pairs = [(wlr2[:, 0:W0], a["L0_gnn_Wl2"]), (wlr2[:, W0:], a["L0_gnn_Wr2"]),
                     (blr2[:, 0:W0], bcast(a["L0_gnn_bl2"], P)), (blr2[:, W0:], bcast(a["L0_gnn_br2"], P)),
                     (wo[:], a["L0_gnn_Wo"]), (bo[:], bcast(a["L0_gnn_bo"], P)),
                     (bias1[:], bcast(a["L0_gnn_bias1"], P)), (bias2[:], bcast(a["L0_gnn_bias2"], P))]
            for c in range(CB):
                pairs.append((att[:, c * W0:(c + 1) * W0], bcast(a["L0_gnn_att2"].rearrange("h c -> (h c)"), P)))
            load(nc, m, "w1", pairs)
            join_chunks(nc, m, "j0", H0, W0, m.pieces0, m.rest0)
            node_groups(nc, m, "n0", H0, W0, m.pieces0, m.rest0, bias1, w=wlr2, cols=2 * W0, bias2=blr2,
                        gathered=m.tl, spread=m.tr, slots=m.edge_rows)
            chunk_rows(nc, m, "cr1", m.tr, m.edge_rows)
            edge_layer(nc, m, "e1", H0, W0, m.tl, m.edge_rows, m.pieces0, att=att, mixer=mixer, tile0=NT // 2)
            join_chunks(nc, m, "j1", H0, W0, m.pieces0, m.rest0)
            node_groups(nc, m, "n1", H0, W0, m.pieces0, m.rest0, bias2, w=wo, cols=D, bias2=bo, last=True)


def feed0(nc, m, a):
    with ExitStack() as st:
        def sb(name, shape, dt=F32):
            return st.enter_context(nc.sbuf_tensor(name, shape, dt))
        xT_all = sb("xT_all", [128, 2, N])
        wr, br, b2 = sb("wr", [P, D]), sb("br", [P, 1]), sb("f_b2", [P, D])
        w1, w2, b1 = sb("f_w1", [128, 2, HID]), sb("f_w2", [128, HID // 128, D]), sb("f_b1", [128, HID // 128])
        wts = sb("wts", [P, NT])
        load(nc, m, "fw", [(wr[:], bcast(a["L0_ffn_wr"].rearrange("d a -> (d a)"), P)), (br[:], bcast(a["L0_ffn_br"], P)),
                           (w1[:], kmaj(a["L0_ffn_w1"])), (w2[:], kmaj(a["L0_ffn_w2"])),
                           (b2[:], bcast(a["L0_ffn_b2"], P)),
                           (b1[:], a["L0_ffn_b1"].rearrange("(j p) -> p j", p=128))])
        norm_stats(nc, m, "ln1")
        route_weights(nc, m, "rw", xT_all, wr, br, wts)
        select_rows(nc, m, "sr", wts)
        feed_forward(nc, m, "ff", xT_all, wts, w1, b1, w2, b2)


@phase
def fold_attention(nc, m, tag, w, att):
    s_p = m.sem(f"{tag}_p")
    with ExitStack() as st:
        prod = st.enter_context(nc.sbuf_tensor(f"{tag}_prod", [128, 2, 2, W1], F32))
        block = st.enter_context(nc.Block())

        @block.vector
        def _(dve):
            for j in range(2):
                dve.tensor_tensor(prod[:, j], w[:, :, 0:W1], att[:, j, :].unsqueeze(1).to_broadcast([128, 2, W1]),
                                  ALU.mult).then_inc(s_p, 1)
                dve.wait_ge(s_p, j + 1)
                for k in range(2):
                    dve.tensor_reduce(w[:, k, W1 + j * H1:W1 + (j + 1) * H1],
                                      prod[:, j, k].rearrange("p (h c) -> p h c", h=H1), AX.X, ALU.add)


def block1(nc, m, a):
    with ExitStack() as st:
        def sb(name, shape, dt=F32):
            return st.enter_context(nc.sbuf_tensor(name, shape, dt))
        norm_stats(nc, m, "ln2")
        with ExitStack() as st2:
            wg = st2.enter_context(nc.sbuf_tensor("wg", [128, 2, W1 + 2 * H1], F32))
            att = st2.enter_context(nc.sbuf_tensor("wg_att", [128, 2, W1], F32))
            load(nc, m, "w2", [(wg[:, :, 0:W1], kmaj(a["w1gat_t"])),
                               (att[:, 0, :], bcast(a["L1_gnn_att_src0"].rearrange("a h c -> (a h c)"), 128)),
                               (att[:, 1, :], bcast(a["L1_gnn_att_dst0"].rearrange("a h c -> (a h c)"), 128))])
            fold_attention(nc, m, "fa", wg, att)
            node_tables(nc, m, "tb1", wg, W1 + 2 * H1, W1 + H1, m.th, m.td, m.edge_rows8)
        with ExitStack() as st2:
            def sb2(name, shape, dt=F32):
                return st2.enter_context(nc.sbuf_tensor(name, shape, dt))
            wqkv, bqkv = sb2("wqkv", [128, 2, 3 * D]), sb2("bqkv", [P, 3 * D])
            wproj, bproj = sb2("wproj", [128, 2, D]), sb2("bproj", [P, D])
            gain = sb2("gain", [P, H1])
            quad, lin, const = sb2("quad", [128, NB, VW1]), sb2("lin", [128, 2, H1 * VW1]), sb2("const", [P, H1 * VW1])
            load(nc, m, "w3", [(wqkv[:], kmaj(a["qkv1_t"])), (bqkv[:], bcast(a["L1_mix_bqkv"], P)),
                               (wproj[:], kmaj(a["proj1_t"])), (bproj[:], bcast(a["L1_mix_bproj"], P)),
                               (gain[:], bcast(a["L1_mix_temperature"].rearrange("a h b c -> (a h b c)"), P))])
            attention_sums(nc, m, "as", wqkv[:, :, D:3 * D], bqkv[:, D:3 * D], quad, lin, const)
            attention_rows(nc, m, "ar", wqkv[:, :, 0:D], bqkv[:, 0:D], gain, quad, lin, const, wproj, bproj)
        chunk_rows(nc, m, "cr2", m.td, m.edge_rows8)
        edge_layer(nc, m, "e2", H1, W1, m.th, m.edge_rows8, m.pieces1)
        bias = sb("bias0", [P, W1])
        load(nc, m, "w4", [(bias[:], bcast(a["L1_gnn_b0"], P))])
        join_chunks(nc, m, "j2", H1, W1, m.pieces1, m.rest1)
        node_groups(nc, m, "n2", H1, W1, m.pieces1, m.rest1, bias, self_loops=(m.th, m.td))


@phase
def prepare_mixer(nc, m, a, mixer, bd, dwc, res, b_res, att):
    s_z, s_ld = m.sem("pm_z"), m.sem("pm_ld")
    with nc.Block() as block:
        @block.vector
        def _(dve):
            dve.memset(mixer.tiny[:], MIN_NORM ** 2)
            dve.memset(mixer.lnmax[:], -log(MAX_ATANH))
            dve.memset(bd[:], 0.0).then_inc(s_z, 1)
            dve.wait_ge(s_ld, 16 * (7 + CB))
            dve.tensor_tensor(bd[:], bd[:], dwc[:].unsqueeze(2).to_broadcast([128, 6, 128]), ALU.mult)

        @block.sync
        def _(sp):
            sp.wait_ge(s_z, 1)
            pwv = a["pw"].rearrange("c (j q r) -> c j q r", q=4, r=32)
            for q in range(4):
                sp.dma_start(bd[32 * q:32 * q + 32, :, 32 * q:32 * q + 32], pwv[:, :, q, :]).then_inc(s_ld, 16)
            with nc.allow_non_contiguous_dma(reason="a column of weights"):
                sp.dma_start(dwc[:], a["dw_taps"][2].rearrange("(j p) -> p j", p=128)).then_inc(s_ld, 16)
            sp.dma_start(res[:], kmaj(a["res_t"])).then_inc(s_ld, 16)
            sp.dma_start(b_res[:], bcast(a["L0_mix_b_res"], P)).then_inc(s_ld, 16)
            load_att(sp, att, a["L0_gnn_att1"], s_ld)
            sp.wait_ge(s_ld, 16 * (7 + CB))


def load_att(sp, att, src, sem):
    for c in range(CB):
        sp.dma_start(att[:, c * W0:(c + 1) * W0], bcast(src.rearrange("h c -> (h c)"), P)).then_inc(sem, 16)


@phase
def chunk_rows(nc, m, tag, table, rows):
    w = table.shape[1]
    s_g, s_o = m.gather_sem(f"{tag}_g"), m.sem(f"{tag}_o")
    with ExitStack() as st:
        first = st.enter_context(nc.sbuf_tensor(f"{tag}_first", [CP, CK, w], F32))
        block = st.enter_context(nc.Block())

        @block.gpsimd
        def _(pool):
            for k in range(CK):
                pool.indirect_dma_start(out=first[:, k, :], out_offset=None, in_=table,
                                        in_offset=bass.IndirectOffsetOnAxis(ap=m.df_i[:, k:k + 1], axis=0)
                                        ).then_inc(s_g, 16)

        @block.sync
        def _(sp):
            sp.wait_ge(s_g, 16 * CK)
            sp.dma_start(rows.rearrange("(k p e) w -> p k e w", k=CK, p=CP)[:, :, 0, :], first[:]).then_inc(s_o, 16)
            sp.wait_ge(s_o, 16)


def layout(z):
    out = {n: v for n, v in z.items() if n not in
           ("src", "L0_mix_w_qkv", "L0_mix_w_dw", "L0_mix_w_pw", "L0_mix_w_res", "L0_ffn_attention_mask",
            "L1_gnn_W0", "L1_gnn_W1", "L1_gnn_att_src1", "L1_gnn_att_dst1", "L1_gnn_b1", "L1_mix_Wqkv", "L1_mix_Wproj")}
    c = np.ascontiguousarray
    out["srcT"] = c(z["src"].reshape(NC, P).T)
    out["dstT"] = c(z["dst"].reshape(NC, P).T)
    out["qkv_taps"] = c(z["L0_mix_w_qkv"].transpose(2, 1, 0))
    out["dw_taps"] = c(z["L0_mix_w_dw"].transpose(2, 1, 0).reshape(5, CV))
    out["pw"] = c(z["L0_mix_w_pw"].reshape(CV, 32).T)
    out["res_t"] = c(z["L0_mix_w_res"].reshape(D, 512).T)
    out["w1gat_t"] = c(z["L1_gnn_W0"].T)
    out["qkv1_t"] = c(z["L1_mix_Wqkv"].T)
    out["proj1_t"] = c(z["L1_mix_Wproj"].T)
    return out


def kernel_program(nc, a, out):
    with ExitStack() as stack:
        m = Mem(nc, stack)
        m.dst = a["dst"]
        setup(nc, m, a)
        block0(nc, m, a)
        feed0(nc, m, a)
        block1(nc, m, a)
        feed1(nc, m, a, out)


def kernel(**inputs):
    import concourse.bacc as _bacc
    from concourse.bass_utils import run_bass_kernel_spmd
    nc = _bacc.Bacc("TRN2", target_bir_lowering=False, num_devices=1)
    arrays, aps = {}, {}
    for name, value in layout(inputs).items():
        arrays[f"in_{name}_dram"] = value
        aps[name] = nc.dram_tensor(f"in_{name}_dram", value.shape, mybir.dt.from_np(value.dtype),
                                   kind="ExternalInput").ap()
    out = nc.dram_tensor("out_0_dram", (N, D), F32, kind="ExternalOutput").ap()
    kernel_program(nc, aps, out)
    r = run_bass_kernel_spmd(nc, [arrays], core_ids=[0])
    return r.results[0]["out_0_dram"]
```
